# Optimizing a Trainium2 kernel written in Bass

```python
import numpy as np
import jax
import jax.numpy as jnp

def _softmax(x, axis=-1):
    return jax.nn.softmax(x, axis=axis)

def _gelu(x):
    return jax.nn.gelu(x, approximate=True)

def _silu(x):
    return jax.nn.silu(x)

def _sigmoid(x):
    return jax.nn.sigmoid(x)

def _layernorm(x, axis=-1, eps=1e-05):
    m = jnp.mean(x, axis=axis, keepdims=True)
    v = jnp.var(x, axis=axis, keepdims=True)
    return (x - m) / jnp.sqrt(v + eps)

def _scatter_add(tgt, idx, src, axis=0):
    return tgt.at[idx].add(src)

def _segment_sum(src, seg, n):
    return jax.ops.segment_sum(src, seg, n)
kernel_name = 'mk_flamingo_gated_d1_seqx_r8_0289f3'

def setup_inputs(seed: int=0):
    np.random.seed(seed)
    _w = jnp.asarray

    def _rec_inputs():
        import jax
        import jax.numpy as jnp
        _rk = jax.random.key(seed)
        x = 7.22e-05 + 1 * jax.random.normal(jax.random.fold_in(_rk, 1), (32, 64, 512), jnp.float32)
        _lenS = 64 - jax.random.randint(jax.random.fold_in(_rk, 7), (32,), 0, max(1, 64 // 4) + 1, jnp.int32)
        _lenS2 = 64 - jax.random.randint(jax.random.fold_in(_rk, 8), (32,), 0, max(1, 64 // 4) + 1, jnp.int32)
        _ctx_4096P = jax.random.normal(jax.random.fold_in(_rk, 11), (32, 16, 512), jnp.float32)
        _ctx_4096c = jax.random.dirichlet(jax.random.fold_in(_rk, 511), 0.3 * jnp.ones((16,), jnp.float32), (32, 64))
        _ctx_4096t = jnp.einsum('bsk,bkd->bsd', _ctx_4096c, _ctx_4096P)
        _ctx_4096t = _ctx_4096t * jax.lax.rsqrt(jnp.mean(jnp.square(_ctx_4096t)) + 1e-12) * 0.953939
        ctx_4096 = 4.13588e-05 + 0.999923 * (_ctx_4096t + 0.3 * jax.random.normal(jax.random.fold_in(_rk, 611), (32, 64, 512), jnp.float32))
        fside_Bx32xSxS2_0 = 1.74963e-06 + 0.0200011 * jax.random.normal(jax.random.fold_in(_rk, 13), (32, 32, 64, 64), jnp.float32)
        _validS = jnp.arange(64)[None, :] < _lenS[:, None]
        _validS2 = jnp.arange(64)[None, :] < _lenS2[:, None]
        _causal = jnp.tril(jnp.ones((64, 64), dtype=bool))
        mask_BxSxS2_bk0 = jnp.logical_not(jnp.broadcast_to(_validS2[:, None, :], (32, 64, 64)))
        _g = jax.random.normal(jax.random.fold_in(_rk, 9001), (2, 1), jnp.float32)
        _g = jnp.sign(_g) * jnp.maximum(jnp.abs(_g), 1.0) + (_g == 0) * 1.0
        g_xattn = _g[0]
        g_ffn = _g[1]
        return (x, ctx_4096, fside_Bx32xSxS2_0, mask_BxSxS2_bk0, g_xattn, g_ffn)
    x, ctx_4096, fside_Bx32xSxS2_0, mask_BxSxS2_bk0, g_xattn, g_ffn = _rec_inputs()

    def _L0_xattn_setup():
        import jax, jax.numpy as jnp
        import numpy as np
        B, S, D, H, DH = (2, 128, 512, 32, 128)
        key = jax.random.key(seed)
        ks = jax.random.split(key, 7)
        hidden_q = jax.random.normal(ks[0], (B, S, D), dtype=jnp.float32)
        hidden_kv = jax.random.normal(ks[1], (B, S, D), dtype=jnp.float32)
        attention_mask = jnp.tril(jnp.ones((B, S, S), dtype=bool))
        position_bias = jax.random.normal(ks[2], (B, H, S, S), dtype=jnp.float32) * 0.02
        Wq = jax.random.normal(ks[3], (D, H * DH), dtype=jnp.float32) * 0.02
        Wk = jax.random.normal(ks[4], (D, H * DH), dtype=jnp.float32) * 0.02
        Wv = jax.random.normal(ks[5], (D, H * DH), dtype=jnp.float32) * 0.02
        Wo = jax.random.normal(ks[6], (H * DH, D), dtype=jnp.float32) * 0.02
        return {'hidden_q': hidden_q, 'hidden_kv': hidden_kv, 'attention_mask': attention_mask, 'position_bias': position_bias, 'Wq': Wq, 'Wk': Wk, 'Wv': Wv, 'Wo': Wo}
    _L0_xattn_all = _L0_xattn_setup()
    _L0_xattn_in = {k: v for k, v in _L0_xattn_all.items() if k in ('Wq', 'Wk', 'Wv', 'Wo')}
    del _L0_xattn_all

    def _L0_ffn_setup():
        import jax, jax.numpy as jnp
        import numpy as np
        LORA_RANK = 16
        LORA_ALPHA = 16
        LORA_SCALE = LORA_ALPHA / LORA_RANK
        key = jax.random.key(seed)
        k1, k2, k3, k4, k5 = jax.random.split(key, 5)
        B, S, D_IN, D_OUT, N_LORA, R = (8, 256, 512, 512, 3, LORA_RANK)
        std = 1.0 / np.sqrt(D_IN)
        x = jax.random.normal(k1, (B, S, D_IN), dtype=jnp.float32)
        weight = jax.random.truncated_normal(k2, -3.0, 3.0, (D_OUT, D_IN), dtype=jnp.float32) * std
        bias = jax.random.normal(k3, (D_OUT,), dtype=jnp.float32) * 0.01
        lora_A = jax.random.normal(k4, (N_LORA, R, D_IN), dtype=jnp.float32) * std
        lora_B = jax.random.normal(k5, (N_LORA, D_OUT, R), dtype=jnp.float32) * 0.02
        lora_start_indices = jnp.arange(4, dtype=jnp.int64) * 2
        return {'x': x, 'weight': weight, 'bias': bias, 'lora_A': lora_A, 'lora_B': lora_B, 'lora_start_indices': lora_start_indices}
    _L0_ffn_all = _L0_ffn_setup()
    _L0_ffn_in = {k: v for k, v in _L0_ffn_all.items() if k in ('weight', 'bias', 'lora_A', 'lora_B', 'lora_start_indices')}
    del _L0_ffn_all
    return {'x': x, 'ctx_4096': ctx_4096, 'fside_Bx32xSxS2_0': fside_Bx32xSxS2_0, 'mask_BxSxS2_bk0': mask_BxSxS2_bk0, 'g_xattn': g_xattn, 'g_ffn': g_ffn, 'L0_xattn_Wq': _L0_xattn_in['Wq'], 'L0_xattn_Wk': _L0_xattn_in['Wk'], 'L0_xattn_Wv': _L0_xattn_in['Wv'], 'L0_xattn_Wo': _L0_xattn_in['Wo'], 'L0_ffn_weight': _L0_ffn_in['weight'], 'L0_ffn_bias': _L0_ffn_in['bias'], 'L0_ffn_lora_A': _L0_ffn_in['lora_A'], 'L0_ffn_lora_B': _L0_ffn_in['lora_B'], 'L0_ffn_lora_start_indices': _L0_ffn_in['lora_start_indices']}

def reference(x, ctx_4096, fside_Bx32xSxS2_0, mask_BxSxS2_bk0, g_xattn, g_ffn, L0_xattn_Wq, L0_xattn_Wk, L0_xattn_Wv, L0_xattn_Wo, L0_ffn_weight, L0_ffn_bias, L0_ffn_lora_A, L0_ffn_lora_B, L0_ffn_lora_start_indices):
    import jax
    import jax.numpy as jnp

    def _L0_xattn_ref(hidden_q, hidden_kv, attention_mask, position_bias, Wq, Wk, Wv, Wo):
        import jax, jax.numpy as jnp
        import numpy as np
        B, S, D, H, DH = (2, 128, 512, 32, 128)
        b, lq, _ = hidden_q.shape
        lk = hidden_kv.shape[1]
        h, dh = (H, DH)
        q = (hidden_q @ Wq).reshape(b, lq, h, dh)
        k = (hidden_kv @ Wk).reshape(b, lk, h, dh)
        v = (hidden_kv @ Wv).reshape(b, lk, h, dh)
        scale = 1.0 / jnp.sqrt(jnp.asarray(dh, dtype=q.dtype))
        score = jnp.einsum('bqhd,bkhd->bhqk', q, k) * scale + position_bias
        mask = attention_mask[:, None, :, :]
        neg_inf = jnp.asarray(-jnp.inf, dtype=score.dtype)
        score = jnp.where(mask, score, neg_inf)
        probs = jax.nn.softmax(score, axis=-1)
        probs = jnp.where(mask, probs, jnp.asarray(0, dtype=probs.dtype))
        ctx = jnp.einsum('bhqk,bkhd->bqhd', probs, v).reshape(b, lq, h * dh)
        return ctx @ Wo

    def _L0_ffn_ref(x, weight, bias, lora_A, lora_B, lora_start_indices):
        import jax, jax.numpy as jnp
        import numpy as np
        LORA_RANK = 16
        LORA_ALPHA = 16
        LORA_SCALE = LORA_ALPHA / LORA_RANK
        y = jnp.einsum('bsd,od->bso', x, weight) + bias
        B = x.shape[0]
        seg = jnp.searchsorted(lora_start_indices, jnp.arange(B), side='right') - 1
        adapter_idx = jnp.clip(seg - 1, 0, lora_A.shape[0] - 1)
        A = lora_A[adapter_idx]
        Bw = lora_B[adapter_idx]
        lo = jnp.einsum('bsr,bor->bso', jnp.einsum('bsd,brd->bsr', x, A), Bw) * LORA_SCALE
        use_lora = (seg > 0)[:, None, None]
        return y + jnp.where(use_lora, lo, jnp.zeros((), dtype=y.dtype))
    x = x + jnp.tanh(g_xattn[0]) * _L0_xattn_ref(_layernorm(x, axis=-1), ctx_4096, mask_BxSxS2_bk0, fside_Bx32xSxS2_0, L0_xattn_Wq, L0_xattn_Wk, L0_xattn_Wv, L0_xattn_Wo)
    x = x + jnp.tanh(g_ffn[0]) * _L0_ffn_ref(_layernorm(x, axis=-1), L0_ffn_weight, L0_ffn_bias, L0_ffn_lora_A, L0_ffn_lora_B, L0_ffn_lora_start_indices)
    return x

_drawn_inputs = setup_inputs


def setup_inputs(seed=0):
    import zlib

    import numpy as np

    out = dict(_drawn_inputs(seed))
    spreads = {}
    factors = {'fside_Bx32xSxS2_0': 26.912, 'L0_ffn_bias': 8.0}
    for name, (base, spread) in spreads.items():
        noise = np.random.default_rng([zlib.crc32(name.encode()), seed]).standard_normal(out[name].shape)
        drawn = base * np.exp(spread * noise) if base else spread * noise
        out[name] = jnp.asarray(drawn.astype(out[name].dtype))
    for name, factor in factors.items():
        out[name] = (out[name] * factor).astype(out[name].dtype)
    return out
```

```python
from contextlib import ExitStack

import numpy as np

import concourse.bass as bass
from concourse import mybir

F32 = mybir.dt.float32
F32R = mybir.dt.float32r
I32 = mybir.dt.int32
U8 = mybir.dt.uint8
ALU = mybir.AluOpType
ACT = mybir.ActivationFunctionType
X = mybir.AxisListType.X

P = 128
NB = 32
S = 64
D = 512
H = 32
DH = 128
NL = 3
R = 16
C = D // P
HALVES = 2
T = NB * S // HALVES
TILES = T // P
BLK = 512
BLOCKS = T // BLK
PB = BLK // P
HG = 2
G = H // HG
STAGES = BLOCKS * HG
SCALE = float(DH) ** -0.5
EPS = 1e-5
MASKED = -1e30
CTX_PIECES = BLOCKS * C
LOADED = CTX_PIECES + C
PIECES = LOADED + 2
STAGE_BUFS = 4


def flamingo_block(nc, x, ctxt, pair_bias, mask, wq, wk, wv, wo, g_xattn, g_ffn, wf, fbias, lora_a, lora_b,
                   lora_starts, lora_const, out):
    with ExitStack() as ctx:
        def sb(name, shape, dt=F32):
            return ctx.enter_context(nc.sbuf_tensor(name, shape, dt))

        def pb(name):
            return ctx.enter_context(nc.psum_tensor(name, [P, 512], F32))

        def sem(name):
            return ctx.enter_context(nc.semaphore(name))

        xt = [sb(f"xt_{p}", [P, C, T], F32R) for p in ("hi", "lo")]
        ct = [sb(f"ct_{p}", [P, C, T], F32R) for p in ("hi", "lo")]
        acc = sb("acc", [P, TILES, D])
        raw_q, raw_k, raw_v = (sb(f"raw_{m}", [P, C, HG * DH]) for m in "qkv")
        raw_o = sb("raw_o", [P, HG, D])
        q_w, k_w, v_w = ([sb(f"w{m}_{p}", [P, C, HG * DH], F32R) for p in ("hi", "lo")] for m in "qkv")
        o_w = [sb(f"wo_{p}", [P, HG, D], F32R) for p in ("hi", "lo")]
        qt = [sb(f"qt_{p}", [P, BLK], F32R) for p in ("hi", "lo")]
        kt = sb("kt", [P, PB, 2, P], F32R)
        v = [[sb(f"v{b}_{p}", [P, PB, HG * DH], F32R) for p in ("hi", "lo")] for b in range(2)]
        ot = [sb(f"ot_{p}", [P, HG, BLK], F32R) for p in ("hi", "lo")]
        pt = sb("pt", [P, PB, 2, P], F32R)
        raw_bias = [sb(f"raw_bias{b}", [P, HG, PB, S]) for b in range(BLOCKS)]
        bias_m = [sb(f"bias_m{b}", [P, PB, S]) for b in range(2)]
        score = sb("score", [P, PB, S])
        shifted = sb("shifted", [P, PB, S])
        score_b = sb("score_b", [P, PB, S])
        attn = sb("attn", [P, BLK])
        expd = sb("expd", [P, PB, S])
        prob = sb("prob", [P, PB, P])
        row_max = sb("row_max", [P, PB])
        row_sum = sb("row_sum", [P, PB])
        row_inv = sb("row_inv", [P, PB])
        row_scale = sb("row_scale", [P, PB])
        mask_u8 = sb("mask_u8", [P, TILES, S], U8)
        mask_add = sb("mask_add", [P, TILES, S])
        row_kept = sb("row_kept", [P, TILES])
        raw_a = sb("raw_a", [P, C, P])
        raw_b = sb("raw_b", [P, D])
        stage = [sb(f"stage{i}", [P, 512]) for i in range(STAGE_BUFS)]
        xn = [sb(f"xn{i}", [P, D]) for i in range(2)]
        stats = sb("stats", [P, TILES, 6])
        mean_var = sb("mean_var", [P, TILES, 2])
        std = sb("std", [P, TILES])
        rstd = sb("rstd", [P, TILES])
        lora_u = sb("lora_u", [P, BLK])
        y_out = [sb(f"y_out{i}", [P, D]) for i in range(2)]
        fb = sb("fb", [P, D])
        ident = sb("ident", [P, P])
        eps = sb("eps", [P, 1])
        g_in = sb("g_in", [P, 2])
        gate = sb("gate", [P, 2])
        starts_i = sb("starts_i", [P, 4], I32)
        starts_f = sb("starts_f", [P, 4])
        lconst = sb("lconst", [P, NB + 1])
        seg = sb("seg", [P, NB])
        seg_j = sb("seg_j", [P, NB])
        use = sb("use", [P, NB])

        f_w = [c[:, :, 0:512] for c in ct]
        a_w = [c[:, :, 512:640] for c in ct]
        b_w = [c[:, :, 640:768] for c in ct]
        lo_t = ot

        q_bank, k_bank = pb("q_bank"), pb("k_bank")
        vo_bank = [pb(f"vo_bank{i}") for i in range(2)]
        s_two = ctx.enter_context(nc.psum_tensor("s_two", [P, PB, 2, P], F32))
        pv_two = ctx.enter_context(nc.psum_tensor("pv_two", [P, PB, 2, P], F32))
        s_half, pv_half = ([two[:, 2 * i:2 * i + 2, :, :].rearrange("p a b c -> p (a b c)") for i in range(2)]
                           for two in (s_two, pv_two))
        t_bank = pv_half[0]
        ln_bank = pv_half
        y_bank = [q_bank, k_bank]
        l_bank = s_half

        raw_q_in, raw_k_in, raw_v_in, raw_o_in = (sem(f"raw_{m}_in") for m in "qkvo")
        bias_in = [sem(f"bias_in{b}") for b in range(BLOCKS)]
        x_in = [sem(f"x_in{i}") for i in range(TILES)]
        stage_in = [sem(f"stage_in{i}") for i in range(STAGE_BUFS)]
        mask_in, gate_in, fb_in, starts_in, const_in = (
            sem(f"{m}_in") for m in ("mask", "gate", "fb", "starts", "const"))
        stored = [sem(f"stored{i}") for i in range(2)]
        q_ps, k_ps, v_ps, s_ps, t_ps, pv_ps, o_ps, xt_ps, lora_ps, y_ps = (
            sem(f"{m}_ps") for m in ("q", "k", "v", "s", "t", "pv", "o", "xt", "lora", "y"))
        q_hi, k_hi, v_hi, pt_hi, ot_b, ot_hi, xt_hi, stage_hi, lora_hi, wq_hi, wk_hi, wv_hi, wo_hi = (
            sem(f"{m}_hi") for m in ("q", "k", "v", "pt", "ot_b", "ot", "xt", "stage", "lora", "wq", "wk", "wv", "wo"))
        q_lo, k_lo, v_lo, pt_lo, ot_lo, xt_lo, stage_lo, lora_lo, wq_lo, wk_lo, wv_lo, wo_lo = (
            sem(f"{m}_lo") for m in ("q", "k", "v", "pt", "ot", "xt", "stage", "lora", "wq", "wk", "wv", "wo"))
        gate_done, exp_done, std_done = sem("gate_done"), sem("exp_done"), sem("std_done")
        score_b_done, score_done, max_done, shift_done, sum_done, inv_done, rscale_done, prob_done = (
            sem(f"{m}_done") for m in ("score_b", "score", "max", "shift", "sum", "inv", "rscale", "prob"))
        ot_sum, acc_done, stats_done, aggr_done, rstd_done, xn_done, u_done, y_done = (
            sem(f"{m}_done") for m in ("ot_sum", "acc", "stats", "aggr", "rstd", "xn", "u", "y"))
        ident_done, zero_done, seg_done, mask_done, kept_done, eps_done, fb_done = (
            sem(f"{m}_done") for m in ("ident", "zero", "seg", "mask", "kept", "eps", "fb"))
        bias_done, yb_done = sem("bias_done"), sem("yb_done")
        lora_a_in, lora_b_in, g1_in = sem("lora_a_in"), sem("lora_b_in"), sem("g1_in")

        def mm3(pe, to, left, right, first, last):
            pe.matmul(to, left[0], right[0], start=first, stop=False)
            pe.matmul(to, left[0], right[1], start=False, stop=False)
            return pe.matmul(to, left[1], right[0], start=False, stop=last)

        def parts(pair, *at):
            return [p[at] for p in pair]

        def cols(i, n):
            return slice(i * n, (i + 1) * n)

        def by(bank, n):
            return bank[:, :].rearrange("p (a b) -> p a b", a=n)

        def both(pe, to, left, right):
            pe.matmul(to, left[0], right, start=True, stop=False)
            return pe.matmul(to, left[1], right, start=False, stop=True)

        def f32(part):
            return part.bitcast(F32)

        block = ctx.enter_context(nc.Block())

        @block.sync
        def _(sp):
            def load(to, src, at, done):
                sp.dma_start(to, src[bass.ds(at, 1)].rearrange("a p f -> (a p) f")).then_inc(done, 16)

            def flat(t):
                return t[:, :, :].rearrange("p a b -> p (a b)")

            def flat4(t):
                return t[:, :, :, :].rearrange("p a b c -> p (a b c)")

            def x_and_context(half, b):
                for j in range(C * b, C * b + C):
                    load(acc[:, j, :], x, TILES * half + j, x_in[j])
                    sp.wait_ge(stage_lo, PIECES * half + max(j - STAGE_BUFS + 1, 0))
                    load(stage[j % STAGE_BUFS][:, :], ctxt, CTX_PIECES * half + j, stage_in[j % STAGE_BUFS])

            def next_group(gg, group, bias_at):
                sp.wait_ge(wq_hi, 2 * gg + 2)
                sp.wait_ge(wq_lo, 2 * gg + 2)
                load(flat(raw_q), wq, group, raw_q_in)
                sp.wait_ge(wk_hi, 2 * gg + 2)
                sp.wait_ge(wk_lo, 2 * gg + 2)
                load(flat(raw_k), wk, group, raw_k_in)
                sp.wait_ge(wv_hi, 2 * gg + 2)
                sp.wait_ge(wv_lo, 2 * gg + 2)
                load(flat(raw_v), wv, group, raw_v_in)
                sp.wait_ge(bias_done, STAGES * gg + 2)
                load(flat4(raw_bias[0]), pair_bias, bias_at, bias_in[0])
                sp.wait_ge(wo_hi, 2 * gg + 2)
                sp.wait_ge(wo_lo, 2 * gg + 2)
                load(flat(raw_o), wo, group, raw_o_in)
                sp.wait_ge(bias_done, STAGES * gg + 4)
                load(flat4(raw_bias[1]), pair_bias, bias_at + 1, bias_in[1])

            sp.dma_start(g_in[:, 0:1], g_xattn.to_broadcast([P, 1])).then_inc(gate_in, 16)
            sp.dma_start(g_in[:, 1:2], g_ffn.to_broadcast([P, 1])).then_inc(g1_in, 16)
            load(flat(raw_q), wq, 0, raw_q_in)
            load(flat(raw_k), wk, 0, raw_k_in)

            with sp.Fori(0, HALVES) as half:
                sp.wait_ge(y_done, TILES * half)
                sp.wait_ge(kept_done, half)
                sp.wait_ge(mask_done, half)
                x_and_context(half, 0)
                sp.dma_start(mask_u8[:, :, :], mask[bass.ds(half, 1)].rearrange("a p b k -> (a p) b k")).then_inc(mask_in, 16)
                x_and_context(half, 1)
                for j in range(CTX_PIECES, LOADED):
                    sp.wait_ge(stage_lo, PIECES * half + j - STAGE_BUFS + 1)
                    load(stage[j % STAGE_BUFS][:, :], wf, j - CTX_PIECES, stage_in[j % STAGE_BUFS])
                with sp.Fori(0, G - 1) as g:
                    next_group(G * half + g, g + 1, BLOCKS * (G * half + g + 1))
                next_group(G * half + (G - 1), 0, half * (-BLOCKS * G) + BLOCKS * G)
                for i in range(TILES):
                    sp.wait_ge(y_done, TILES * half + i + 1)
                    sp.dma_start(out[bass.ds(TILES * half + i, 1)].rearrange("a p f -> (a p) f"),
                                 y_out[i % 2][:, :]).then_inc(stored[i % 2], 16)
            for b in range(2):
                sp.wait_ge(stored[b], 16 * HALVES * TILES // 2)

        @block.tensor
        def _(pe):
            def v_tiles(t, u, grp, tb):
                bank = vo_bank[u]
                pe.wait_ge(wv_lo, 2 * grp + 2)
                for i in range(2):
                    tile = PB * tb + 2 * u + i
                    for c in range(C):
                        mm = mm3(pe, bank[:, cols(i, 256)], parts(ct, slice(None), c, cols(tile, P)),
                                 parts(v_w, slice(None), c, slice(None)), c == 0, c == C - 1)
                mm.then_inc(v_ps, 1)

            def out_tile(p):
                bank = vo_bank[p % 2]
                for h in range(HG):
                    mm = mm3(pe, bank[:, :], parts(ot, slice(None), h, cols(p, P)),
                             parts(o_w, slice(None), h, slice(None)), h == 0, h == HG - 1)
                mm.then_inc(o_ps, 1)

            def slot(gg, s, now=True, before=True, first=False, out_before=True):
                n, t, grp = STAGES * gg + s, BLOCKS * gg + s // 2, gg + s // STAGES
                h, tb = s % HG, s // 2 % BLOCKS
                if now:
                    tokens = cols(tb, BLK)
                    for w, w_lo, src, bank, lo, done in ((q_w, wq_lo, xt, q_bank, q_lo, q_ps),
                                                         (k_w, wk_lo, ct, k_bank, k_lo, k_ps)):
                        pe.wait_ge(w_lo, 2 * grp + 1 + h)
                        pe.wait_ge(lo, n)
                        for c in range(C):
                            mm = mm3(pe, bank[:, :], parts(w, slice(None), c, cols(h, DH)),
                                     parts(src, slice(None), c, tokens), c == 0, c == C - 1)
                        mm.then_inc(done, 1)

                def block_product(u):
                    if s % 2 == 0 and now:
                        if u == 0 and not first:
                            pe.wait_ge(acc_done, PB * (t - 1))
                        v_tiles(t, u, grp, tb)
                    if s % 2 == 1 and out_before:
                        if u == 0:
                            pe.wait_ge(ot_lo, n - 1)
                            pe.wait_ge(wo_lo, 2 * (gg + (s // 2 - 1) // 2) + 2)
                        for p in (2 * u, 2 * u + 1):
                            if p < 2 and now:
                                pe.wait_ge(v_lo, 2 * t + p + 1)
                            if p >= 2 or not now:
                                pe.wait_ge(acc_done, PB * (t - 1) + p - 1)
                            out_tile(p)

                block_product(0)
                if before:
                    pe.wait_ge(prob_done, n)
                    pe.wait_ge(ot_sum, n - 1)
                    for p in range(PB):
                        mm = pe.transpose(t_bank[:, cols(p, P)], prob[:, p, :], ident[:, :])
                    mm.then_inc(t_ps, 1)
                block_product(1)
                if now:
                    pe.wait_ge(q_lo, n + 1)
                    pe.wait_ge(k_lo, n + 1)
                    pe.wait_ge(score_done, n)
                    for p in range(PB):
                        mm = both(pe, s_two[:, p, :, :], parts(qt, slice(None), cols(p, P)), kt[:, p, :, :])
                    mm.then_inc(s_ps, 1)
                if before:
                    vb, vh = v[(s - 1) // 2 % 2], (s - 1) % HG
                    pe.wait_ge(v_lo, 2 * (BLOCKS * gg + (s - 1) // 2) + 2)
                    pe.wait_ge(pt_lo, n)
                    for p in range(PB):
                        mm = both(pe, pv_two[:, p, :, :], parts(vb, slice(None), p, cols(vh, DH)), pt[:, p, :, :])
                    mm.then_inc(pv_ps, 1)

            def transposes(run, i):
                pe.wait_ge(xn_done, TILES * run + i + 1)
                pe.wait_ge(xt_lo, TILES * run + max(i - 1, 0))
                for c in range(C):
                    mm = pe.transpose(ln_bank[i % 2][:, cols(c, P)], xn[i % 2][:, cols(c, P)], ident[:, :])
                mm.then_inc(xt_ps, 1)

            def lora_inner(half, b):
                pe.wait_ge(xt_lo, TILES * (2 * half + 1) + PB * (b + 1))
                for c in range(C):
                    mm = mm3(pe, l_bank[b][:, :], parts(a_w, slice(None), c, slice(None)),
                             parts(xt, slice(None), c, cols(b, BLK)), c == 0, c == C - 1)
                mm.then_inc(lora_ps, 1)

            def dense(half, i):
                pe.wait_ge(y_done, TILES * half + max(i - 1, 0))
                pe.wait_ge(lora_lo, BLOCKS * half + i // PB + 1)
                for c in range(C):
                    mm3(pe, y_bank[i % 2][:, :], parts(xt, slice(None), c, cols(i, P)),
                        parts(f_w, slice(None), c, slice(None)), c == 0, False)
                mm3(pe, y_bank[i % 2][:, :], parts(lo_t, slice(None), i // PB, cols(i % PB, P)), b_w,
                    False, True).then_inc(y_ps, 1)

            pe.wait_ge(ident_done, 2)
            with pe.Fori(0, HALVES) as half:
                for i in range(PB):
                    transposes(2 * half, i)
                pe.wait_ge(stage_lo, PIECES * half + C)
                pe.wait_ge(xt_lo, 2 * TILES * half + PB)
                slot(G * half, 0, before=False, first=True)
                for i in range(PB, TILES):
                    transposes(2 * half, i)
                pe.wait_ge(stage_lo, PIECES * half + CTX_PIECES)
                pe.wait_ge(xt_lo, 2 * TILES * half + TILES)
                slot(G * half, 1, out_before=False)
                with pe.Fori(0, G - 1) as g:
                    for s in range(2, STAGES + 2):
                        slot(G * half + g, s)
                slot(G * half + (G - 1), 2)
                slot(G * half + (G - 1), 3)
                slot(G * half + (G - 1), 4, now=False)
                slot(G * half + (G - 1), 5, now=False, before=False)
                for i in range(PB):
                    transposes(2 * half + 1, i)
                pe.wait_ge(stage_lo, PIECES * half + PIECES)
                lora_inner(half, 0)
                for i in range(PB, TILES):
                    transposes(2 * half + 1, i)
                for i in range(PB):
                    dense(half, i)
                lora_inner(half, 1)
                for i in range(PB, TILES):
                    dense(half, i)

        @block.scalar
        def _(act):
            def hi(to, src, done, func=ACT.Copy, **kw):
                act.activation(to, src, func, **kw).then_inc(done, 1)

            def weights_qk(grp, h):
                for raw, arrived, to, ps, done in ((raw_q, raw_q_in, q_w, q_ps, wq_hi),
                                                   (raw_k, raw_k_in, k_w, k_ps, wk_hi)):
                    act.wait_ge(arrived, 16 * (grp + 1))
                    if h == 1:
                        act.wait_ge(ps, STAGES * grp)
                    hi(to[0][:, :, cols(h, DH)], raw[:, :, cols(h, DH)], done)

            def weights_v(grp):
                act.wait_ge(raw_v_in, 16 * (grp + 1))
                for u in range(2):
                    hi(v_w[0][:, cols(u, 2), :], raw_v[:, cols(u, 2), :], wv_hi)

            def weights_o(grp):
                act.wait_ge(raw_o_in, 16 * (grp + 1))
                act.wait_ge(o_ps, BLOCKS * PB * grp)
                for u in range(HG):
                    hi(o_w[0][:, u, :], raw_o[:, u, :], wo_hi, scale=gate[:, 0:1])

            def slot(gg, s, now=True, before=True, first=False):
                n, t, grp = STAGES * gg + s, BLOCKS * gg + s // 2, gg + s // STAGES
                tb = s // 2 % BLOCKS
                if now:
                    act.wait_ge(s_ps, n)
                    act.wait_ge(q_ps, n + 1)
                    hi(qt[0][:, :], q_bank[:, :], q_hi)
                    act.wait_ge(k_ps, n + 1)
                    hi(kt[:, :, 0, :], by(k_bank, PB), k_hi)
                    if s % STAGES == 0:
                        weights_qk(grp, 1)
                    if s % STAGES == 2:
                        weights_qk(grp + 1, 0)
                        weights_o(grp)
                    if s % STAGES == 3:
                        weights_v(grp + 1)
                if now and s % 2 == 0:
                    if not first:
                        act.wait_ge(pv_ps, 2 * (t - 1))
                    act.wait_ge(v_ps, 2 * t + 1)
                    hi(v[tb][0][:, 0:2, :], by(vo_bank[0], 2), v_hi)
                if before:
                    act.wait_ge(pv_ps, n - 1)
                    act.wait_ge(t_ps, n)
                    hi(pt[:, :, 0, :], by(t_bank, PB), pt_hi)
                if now and s % 2 == 0:
                    act.wait_ge(v_ps, 2 * t + 2)
                    hi(v[tb][0][:, 2:4, :], by(vo_bank[1], 2), v_hi)
                if before:
                    act.wait_ge(ot_lo, n - 1)
                    act.wait_ge(pv_ps, n)
                    act.activation(by(attn, PB), pv_two[:, :, 1, :], ACT.Copy).then_inc(ot_b, 1)
                    act.wait_ge(o_ps, PB * (BLOCKS * gg + (s - 1) // 2))
                    act.wait_ge(ot_sum, n)
                    hi(ot[0][:, (s - 1) % HG, :], attn[:, :], ot_hi)
                if now:
                    act.wait_ge(sum_done, n)
                    act.wait_ge(prob_done, n)
                    act.wait_ge(shift_done, n + 1)
                    hi(expd[:, :, :], shifted[:, :, :], exp_done, ACT.Exp)

            def deviations(run, b):
                act.wait_ge(aggr_done, TILES * run + PB * (b + 1))
                act.activation(std[:, cols(b, PB)], mean_var[:, cols(b, PB), 1], ACT.Sqrt,
                               bias=eps[:, 0:1]).then_inc(std_done, 1)

            def turned(run, i):
                act.wait_ge(xt_ps, TILES * run + i + 1)
                hi(xt[0][:, :, cols(i, P)], by(ln_bank[i % 2], C), xt_hi)

            def stage_loaded(half, j):
                act.wait_ge(stage_in[j % STAGE_BUFS], 16 * (LOADED // STAGE_BUFS * half + j // STAGE_BUFS + 1))

            def context_piece(half, j):
                stage_loaded(half, j)
                hi(ct[0][:, j % C, cols(j // C, BLK)], stage[j % STAGE_BUFS][:, :], stage_hi)

            act.wait_ge(gate_in, 16)
            act.wait_ge(g1_in, 16)
            act.activation(gate[:, :], g_in[:, :], ACT.Tanh).then_inc(gate_done, 1)
            act.wait_ge(eps_done, 1)
            act.dma_start(raw_v[:, :, :].rearrange("p a b -> p (a b)"), wv[0]).then_inc(raw_v_in, 16)
            act.dma_start(raw_bias[0][:, :, :, :].rearrange("p a b c -> p (a b c)"), pair_bias[0]).then_inc(bias_in[0], 16)
            act.dma_start(raw_o[:, :, :].rearrange("p a b -> p (a b)"), wo[0]).then_inc(raw_o_in, 16)
            act.dma_start(raw_bias[1][:, :, :, :].rearrange("p a b c -> p (a b c)"), pair_bias[1]).then_inc(bias_in[1], 16)
            act.dma_start(starts_i[:, :], lora_starts.to_broadcast([P, NL + 1])).then_inc(starts_in, 16)
            act.dma_start(lconst[:, :], lora_const).then_inc(const_in, 16)
            act.dma_start(fb[:, :], fbias.to_broadcast([P, D])).then_inc(fb_in, 16)
            act.wait_ge(zero_done, 3)
            act.dma_start(raw_a[:, :, 0:NL * R], lora_a).then_inc(lora_a_in, 16)
            act.dma_start(raw_b[0:NL * R, :], lora_b).then_inc(lora_b_in, 16)
            weights_qk(0, 0)
            act.wait_ge(gate_done, 1)
            weights_v(0)
            with act.Fori(0, HALVES) as half:
                act.wait_ge(y_ps, TILES * half)
                for j in range(C):
                    context_piece(half, j)
                deviations(2 * half, 0)
                for i in range(PB):
                    turned(2 * half, i)
                deviations(2 * half, 1)
                slot(G * half, 0, before=False, first=True)
                for j in range(C, CTX_PIECES):
                    context_piece(half, j)
                for i in range(PB, TILES):
                    turned(2 * half, i)
                slot(G * half, 1)
                with act.Fori(0, G - 1) as g:
                    for s in range(2, STAGES + 2):
                        slot(G * half + g, s)
                slot(G * half + (G - 1), 2)
                slot(G * half + (G - 1), 3)
                act.wait_ge(v_ps, 2 * BLOCKS * G * (half + 1))
                act.wait_ge(k_ps, STAGES * G * (half + 1))
                for j in range(CTX_PIECES, LOADED):
                    stage_loaded(half, j)
                    hi(f_w[0][:, j - CTX_PIECES, :], stage[j % STAGE_BUFS][:, :], stage_hi, scale=gate[:, 1:2])
                act.wait_ge(lora_a_in, 16)
                hi(a_w[0], raw_a[:, :, :], stage_hi)
                act.wait_ge(lora_b_in, 16)
                hi(b_w[0], raw_b[:, :].rearrange("p (a b) -> p a b", a=C), stage_hi, scale=gate[:, 1:2])
                slot(G * half + (G - 1), 4, now=False)
                act.wait_ge(q_ps, STAGES * G * (half + 1))
                for b in range(BLOCKS):
                    deviations(2 * half + 1, b)
                for b in range(BLOCKS):
                    for i in range(PB * b, PB * b + PB):
                        turned(2 * half + 1, i)
                    if b == 0:
                        act.wait_ge(o_ps, PB * BLOCKS * G * (half + 1))
                        act.wait_ge(u_done, BLOCKS * half + 1)
                        hi(lo_t[0][:, 0, :], lora_u[:, :], lora_hi)
                act.wait_ge(u_done, BLOCKS * half + 2)
                hi(lo_t[0][:, 1, :], lora_u[:, :], lora_hi)

        @block.vector
        def _(dve):
            def lo(to, src, of, done):
                dve.tensor_tensor(to, src, f32(of), ALU.subtract).then_inc(done, 1)

            def lo_scaled(to, src, scale, of, done):
                dve.scalar_tensor_tensor(out=to, in0=src, scalar=scale, in1=f32(of), op0=ALU.mult,
                                         op1=ALU.subtract).then_inc(done, 1)

            def slot(gg, s, now=True, before=True, out_before=True):
                n, t, grp = STAGES * gg + s, BLOCKS * gg + s // 2, gg + s // STAGES
                tb = s // 2 % BLOCKS
                if now:
                    dve.wait_ge(q_hi, n + 1)
                    lo(qt[1][:, :], q_bank[:, :], qt[0][:, :], q_lo)
                    dve.wait_ge(k_hi, n + 1)
                    lo(kt[:, :, 1, :], by(k_bank, PB), kt[:, :, 0, :], k_lo)
                    if s % STAGES == 2:
                        for u in range(HG):
                            dve.wait_ge(wo_hi, 2 * grp + 1 + u)
                            lo_scaled(o_w[1][:, u, :], raw_o[:, u, :], gate[:, 0:1], o_w[0][:, u, :], wo_lo)

                def block_product(u):
                    if now and s % 2 == 0:
                        dve.wait_ge(v_hi, 2 * t + 1 + u)
                        lo(v[tb][1][:, cols(u, 2), :], by(vo_bank[u], 2), v[tb][0][:, cols(u, 2), :], v_lo)
                    if out_before and s % 2 == 1:
                        if u == 0:
                            dve.wait_ge(acc_done, PB * (t - 1))
                        for p in (2 * u, 2 * u + 1):
                            dve.wait_ge(o_ps, PB * (t - 1) + p + 1)
                            tile = PB * ((s // 2 - 1) % BLOCKS) + p
                            dve.tensor_tensor(acc[:, tile, :], vo_bank[p % 2][:, :], acc[:, tile, :],
                                              ALU.add).then_inc(acc_done, 1)

                block_product(0)
                if before:
                    dve.wait_ge(pt_hi, n)
                    lo(pt[:, :, 1, :], by(t_bank, PB), pt[:, :, 0, :], pt_lo)
                block_product(1)
                if now:
                    dve.wait_ge(bias_done, n + 1)
                    dve.wait_ge(shift_done, n)
                    dve.wait_ge(s_ps, n + 1)
                    for part, to, plus, done in ((1, score_b, bias_m[s % 2], score_b_done),
                                                 (0, score, score_b, score_done)):
                        for b in range(2):
                            rows = cols(b, S)
                            last = dve.scalar_tensor_tensor(out=to[rows, :, :], in0=s_two[rows, :, part, rows],
                                                            scalar=SCALE, in1=plus[rows, :, :],
                                                            op0=ALU.mult, op1=ALU.add)
                        last.then_inc(done, 1)
                        dve.wait_ge(done, n + 1)
                    dve.tensor_reduce(row_max[:, :], score[:, :, :], X, ALU.max).then_inc(max_done, 1)
                if before:
                    dve.wait_ge(ot_b, n)
                    dve.tensor_tensor(by(attn, PB), pv_two[:, :, 0, :], by(attn, PB), ALU.add).then_inc(ot_sum, 1)
                if now:
                    dve.wait_ge(exp_done, n + 1)
                    dve.tensor_reduce(row_sum[:, :], expd[:, :, :], X, ALU.add).then_inc(sum_done, 1)
                    dve.wait_ge(sum_done, n + 1)
                    dve.reciprocal(row_inv[:, :], row_sum[:, :]).then_inc(inv_done, 1)
                    dve.wait_ge(inv_done, n + 1)
                    dve.tensor_tensor(row_scale[:, :], row_inv[:, :], row_kept[:, cols(tb, PB)],
                                      ALU.mult).then_inc(rscale_done, 1)

            def statistics(run, b):
                for i in range(PB * b, PB * b + PB):
                    dve.bn_stats(stats[:, i, :], acc[:, i, :]).then_inc(stats_done, 1)
                all_four = TILES * run + PB * (b + 1)
                dve.lower_val(all_four)
                dve.wait_ge(seg_done, 1)
                dve.wait_ge(stats_done, all_four)
                for i in range(PB * b, PB * b + PB):
                    dve.bn_aggr(mean_var[:, i, :], stats[:, i, :]).then_inc(aggr_done, 1)

            def invert(run, b):
                dve.wait_ge(std_done, BLOCKS * run + b + 1)
                dve.reciprocal(rstd[:, cols(b, PB)], std[:, cols(b, PB)]).then_inc(rstd_done, 1)
                dve.wait_ge(rstd_done, BLOCKS * run + b + 1)

            def normalise(run, i):
                dve.wait_ge(xt_ps, TILES * run + max(i - 1, 0))
                dve.tensor_scalar(xn[i % 2][:, :], acc[:, i, :], mean_var[:, i, 0:1], rstd[:, i:i + 1],
                                  ALU.subtract, ALU.mult).then_inc(xn_done, 1)

            def turned(run, i):
                dve.wait_ge(xt_hi, TILES * run + i + 1)
                lo(xt[1][:, :, cols(i, P)], by(ln_bank[i % 2], C), xt[0][:, :, cols(i, P)], xt_lo)

            def norm_tiles(run, b):
                for i in range(PB * b, PB * b + PB):
                    normalise(run, i)
                    if i > PB * b:
                        turned(run, i - 1)
                turned(run, PB * b + PB - 1)

            def lora_use(half, b):
                dve.wait_ge(lora_ps, BLOCKS * half + b + 1)
                dve.wait_ge(seg_done, 2 * NL + 3)
                batches = use[:, bass.ds(2 * TILES * half + 2 * PB * b, 2 * PB)]
                dve.tensor_tensor(lora_u[:, :].rearrange("p (b s) -> p b s", b=2 * PB), by(l_bank[b], 2 * PB),
                                  batches.unsqueeze(2).to_broadcast([P, 2 * PB, S]), ALU.mult).then_inc(u_done, 1)
                dve.wait_ge(lora_hi, BLOCKS * half + b + 1)
                lo(lo_t[1][:, b, :], lora_u[:, :], lo_t[0][:, b, :], lora_lo)

            def context_piece(half, j):
                dve.wait_ge(stage_hi, PIECES * half + j + 1)
                at = (slice(None), j % C, cols(j // C, BLK))
                lo(ct[1][at], stage[j % STAGE_BUFS][:, :], ct[0][at], stage_lo)

            dve.memset(eps[:, :], EPS).then_inc(eps_done, 1)
            dve.memset(prob[:, :, :], 0.0).then_inc(zero_done, 1)
            dve.memset(raw_a[:, :, :], 0.0).then_inc(zero_done, 1)
            dve.memset(raw_b[:, :], 0.0).then_inc(zero_done, 1)
            dve.wait_ge(gate_done, 1)
            dve.wait_ge(fb_in, 16)
            dve.tensor_scalar(fb[:, :], fb[:, :], gate[:, 1:2], None, ALU.mult).then_inc(fb_done, 1)
            dve.wait_ge(starts_in, 16)
            dve.wait_ge(const_in, 16)
            dve.tensor_copy(starts_f[:, :], starts_i[:, :]).then_inc(seg_done, 1)
            dve.wait_ge(seg_done, 1)
            dve.tensor_scalar(seg[:, :], lconst[:, 0:NB], starts_f[:, 0:1], None, ALU.is_ge).then_inc(seg_done, 1)
            for j in range(1, NL + 1):
                dve.wait_ge(seg_done, 2 * j)
                dve.tensor_scalar(seg_j[:, :], lconst[:, 0:NB], starts_f[:, j:j + 1], None, ALU.is_ge).then_inc(seg_done, 1)
                dve.wait_ge(seg_done, 2 * j + 1)
                dve.tensor_tensor(seg[:, :], seg[:, :], seg_j[:, :], ALU.add).then_inc(seg_done, 1)
            dve.wait_ge(seg_done, 2 * NL + 2)
            dve.tensor_scalar(use[:, :], seg[:, :], lconst[:, NB:NB + 1], None, ALU.is_equal).then_inc(seg_done, 1)
            with dve.Fori(0, HALVES) as half:
                for i in range(PB):
                    dve.wait_ge(x_in[i], 16 * (half + 1))
                statistics(2 * half, 0)
                for j in range(C):
                    context_piece(half, j)
                invert(2 * half, 0)
                norm_tiles(2 * half, 0)
                for i in range(PB, TILES):
                    dve.wait_ge(x_in[i], 16 * (half + 1))
                statistics(2 * half, 1)
                dve.wait_ge(mask_in, 16 * (half + 1))
                dve.tensor_reduce(row_kept[:, :], mask_u8[:, :, :], X, ALU.max).then_inc(kept_done, 1)
                dve.wait_ge(kept_done, half + 1)
                slot(G * half, 0, before=False)
                for j in range(C, CTX_PIECES):
                    context_piece(half, j)
                invert(2 * half, 1)
                norm_tiles(2 * half, 1)
                slot(G * half, 1, out_before=False)
                with dve.Fori(0, G - 1) as g:
                    for s in range(2, STAGES + 2):
                        slot(G * half + g, s)
                slot(G * half + (G - 1), 2)
                slot(G * half + (G - 1), 3)
                for j in range(CTX_PIECES, LOADED):
                    dve.wait_ge(stage_hi, PIECES * half + j + 1)
                    c = j - CTX_PIECES
                    lo_scaled(f_w[1][:, c, :], stage[j % STAGE_BUFS][:, :], gate[:, 1:2], f_w[0][:, c, :], stage_lo)
                dve.wait_ge(stage_hi, PIECES * half + LOADED + 1)
                lo(a_w[1], raw_a[:, :, :], a_w[0], stage_lo)
                dve.wait_ge(stage_hi, PIECES * half + LOADED + 2)
                lo_scaled(b_w[1], raw_b[:, :].rearrange("p (a b) -> p a b", a=C), gate[:, 1:2], b_w[0], stage_lo)
                slot(G * half + (G - 1), 4, now=False)
                slot(G * half + (G - 1), 5, now=False, before=False)
                run = 2 * half + 1
                dve.wait_ge(acc_done, PB * BLOCKS * G * (half + 1))
                for b in range(BLOCKS):
                    statistics(run, b)
                for b in range(BLOCKS):
                    invert(run, b)
                for b in range(BLOCKS):
                    norm_tiles(run, b)
                    if b == 1:
                        continue
                    lora_use(half, b)
                for i in range(TILES):
                    if i == PB:
                        lora_use(half, 1)
                    dve.wait_ge(y_ps, TILES * half + i + 1)
                    dve.wait_ge(yb_done, TILES * half + i + 1)
                    dve.wait_ge(stored[i % 2], 16 * (TILES // 2 * half + i // 2))
                    dve.tensor_tensor(y_out[i % 2][:, :], y_bank[i % 2][:, :], acc[:, i, :],
                                      ALU.add).then_inc(y_done, 1)

        @block.gpsimd
        def _(pool):
            def lo(to, src, of, done):
                pool.tensor_tensor(to, src, f32(of), ALU.subtract).then_inc(done, 1)

            def weights_qk(grp, h):
                for raw, w, w_hi, w_lo in ((raw_q, q_w, wq_hi, wq_lo), (raw_k, k_w, wk_hi, wk_lo)):
                    pool.wait_ge(w_hi, 2 * grp + 1 + h)
                    at = (slice(None), slice(None), cols(h, DH))
                    lo(w[1][at], raw[at], w[0][at], w_lo)

            def weights_v(grp):
                for u in range(2):
                    pool.wait_ge(wv_hi, 2 * grp + 1 + u)
                    lo(v_w[1][:, cols(u, 2), :], raw_v[:, cols(u, 2), :], v_w[0][:, cols(u, 2), :], wv_lo)

            def attention_lo(n, s):
                pool.wait_ge(ot_hi, n)
                lo(ot[1][:, (s - 1) % HG, :], attn[:, :], ot[0][:, (s - 1) % HG, :], ot_lo)

            def slot(gg, s, first=False):
                n, grp = STAGES * gg + s, gg + s // STAGES
                tb = s // 2 % BLOCKS
                pool.wait_ge(prob_done, n)
                pool.wait_ge(bias_in[tb], 16 * (grp + 1))
                if not first:
                    pool.wait_ge(score_done, n - 1)
                pool.tensor_tensor(bias_m[s % 2][:, :, :], raw_bias[tb][:, s % HG, :, :],
                                   mask_add[:, cols(tb, PB), :], ALU.add).then_inc(bias_done, 1)
                if s % STAGES == 0:
                    weights_qk(grp, 1)
                if s % STAGES == 2:
                    weights_qk(grp + 1, 0)
                if s % STAGES == 3:
                    weights_v(grp + 1)
                pool.wait_ge(exp_done, n)
                pool.wait_ge(max_done, n + 1)
                pool.tensor_tensor(shifted[:, :, :], score[:, :, :],
                                   row_max[:, :].unsqueeze(2).to_broadcast([P, PB, S]),
                                   ALU.subtract).then_inc(shift_done, 1)
                if not first:
                    attention_lo(n, s)
                if not first:
                    pool.wait_ge(ot_lo, n)
                pool.wait_ge(t_ps, n)
                pool.wait_ge(rscale_done, n + 1)
                for b in range(2):
                    rows = cols(b, S)
                    last = pool.tensor_tensor(prob[rows, :, rows], expd[rows, :, :],
                                              row_scale[rows, :].unsqueeze(2).to_broadcast([S, PB, S]), ALU.mult)
                last.then_inc(prob_done, 1)

            pool.memset(ident[:, :], 0.0).then_inc(ident_done, 1)
            pool.wait_ge(ident_done, 1)
            pool.affine_select(out=ident[:, :], in_=ident[:, :], compare_op=ALU.not_equal, fill=1.0, base=0,
                               pattern=[[-1, P]], channel_multiplier=1).then_inc(ident_done, 1)
            weights_qk(0, 0)
            weights_v(0)
            with pool.Fori(0, HALVES) as half:
                mask_loads = 16 * (half + 1)
                pool.lower_val(mask_loads)
                pool.wait_ge(zero_done, 1)
                pool.wait_ge(mask_in, mask_loads)
                pool.tensor_scalar(mask_add[:, :, :], mask_u8[:, :, :], -1.0, -MASKED, ALU.add,
                                   ALU.mult).then_inc(mask_done, 1)
                pool.wait_ge(mask_done, half + 1)
                slot(G * half, 0, first=True)
                slot(G * half, 1)
                with pool.Fori(0, G - 1) as g:
                    for s in range(2, STAGES + 2):
                        slot(G * half + g, s)
                slot(G * half + (G - 1), 2)
                slot(G * half + (G - 1), 3)
                pool.wait_ge(prob_done, STAGES * G * (half + 1))
                attention_lo(STAGES * G * (half + 1), STAGES)
                pool.wait_ge(fb_done, 1)
                for i in range(TILES):
                    pool.wait_ge(xn_done, TILES * (2 * half + 1) + i + 1)
                    pool.tensor_tensor(acc[:, i, :], acc[:, i, :], fb[:, :], ALU.add).then_inc(yb_done, 1)


_OUTS = [((NB, S, D), "float32")]


def kernel(**inputs):
    import numpy as _np
    import concourse.bacc as _bacc
    from concourse import mybir as _mybir
    from concourse.bass_utils import run_bass_kernel_spmd as _run

    a = {k: _np.asarray(v) for k, v in inputs.items()}

    def by_group(w):
        return w.reshape(C, P, G, HG * DH).transpose(2, 1, 0, 3).reshape(G, P, C * HG * DH)

    bias = a["fside_Bx32xSxS2_0"].reshape(HALVES, BLOCKS, PB, 2, G, HG, S, S)
    mask = a["mask_BxSxS2_bk0"].reshape(HALVES, TILES, 2, S, S)
    arrays = {
        "x": a["x"].reshape(HALVES * TILES, P, D),
        "ctxt": a["ctx_4096"].reshape(HALVES, BLOCKS, BLK, C, P).transpose(0, 1, 3, 4, 2).reshape(-1, P, BLK),
        "pair_bias": bias.transpose(0, 4, 1, 3, 6, 5, 2, 7).reshape(HALVES * G * BLOCKS, P, HG * PB * S),
        "mask": mask.transpose(0, 2, 3, 1, 4).reshape(HALVES, P, TILES, S),
        "wq": by_group(a["L0_xattn_Wq"]),
        "wk": by_group(a["L0_xattn_Wk"]),
        "wv": by_group(a["L0_xattn_Wv"]),
        "wo": a["L0_xattn_Wo"].reshape(G, HG, DH, D).transpose(0, 2, 1, 3).reshape(G, P, HG * D),
        "g_xattn": a["g_xattn"].reshape(1, 1),
        "g_ffn": a["g_ffn"].reshape(1, 1),
        "wf": a["L0_ffn_weight"].T.reshape(C, P, D),
        "fbias": a["L0_ffn_bias"].reshape(1, D),
        "lora_a": a["L0_ffn_lora_A"].reshape(NL * R, C, P).transpose(2, 1, 0),
        "lora_b": a["L0_ffn_lora_B"].transpose(0, 2, 1).reshape(NL * R, D),
        "lora_starts": a["L0_ffn_lora_start_indices"].reshape(1, NL + 1),
        "lora_const": _np.concatenate([_np.tile(_np.arange(NB, dtype=_np.float32), (P, 1)),
                                       (_np.arange(P)[:, None] // R + 2).astype(_np.float32)], axis=1),
    }
    arrays = {f"in_{k}": _np.ascontiguousarray(v) for k, v in arrays.items()}
    nc = _bacc.Bacc("TRN2", target_bir_lowering=False, num_devices=1)
    args = [nc.dram_tensor(k, v.shape, _mybir.dt.from_np(v.dtype), kind="ExternalInput").ap()
            for k, v in arrays.items()]
    args.append(nc.dram_tensor("out_0", (HALVES * TILES, P, D), _mybir.dt.float32, kind="ExternalOutput").ap())
    flamingo_block(nc, *args)
    r = _run(nc, [arrays], core_ids=[0])
    return r.results[0]["out_0"].reshape(_OUTS[0][0])
```

```python
from contextlib import ExitStack

import numpy as np

import concourse.bass as bass
from concourse import mybir

F32 = mybir.dt.float32
F32R = mybir.dt.float32r
I32 = mybir.dt.int32
U8 = mybir.dt.uint8
ALU = mybir.AluOpType
ACT = mybir.ActivationFunctionType
X = mybir.AxisListType.X

P = 128
NB = 32
S = 64
D = 512
H = 32
DH = 128
NL = 3
R = 16
C = D // P
HALVES = 2
T = NB * S // HALVES
TILES = T // P
BLK = 512
BLOCKS = T // BLK
PB = BLK // P
HG = 2
G = H // HG
STAGES = BLOCKS * HG
SCALE = float(DH) ** -0.5
EPS = 1e-5
MASKED = -1e30
CTX_PIECES = BLOCKS * C
PIECES = CTX_PIECES + C
STAGE_BUFS = 4


def flamingo_block(nc, x, ctxt, pair_bias, mask, wq, wk, wv, wo, g_xattn, g_ffn, wf, fbias, lora_a, lora_b,
                   lora_starts, lora_const, out):
    with ExitStack() as ctx:
        def sb(name, shape, dt=F32):
            return ctx.enter_context(nc.sbuf_tensor(name, shape, dt))

        def pb(name):
            return ctx.enter_context(nc.psum_tensor(name, [P, 512], F32))

        def sem(name):
            return ctx.enter_context(nc.semaphore(name))

        xt = [sb(f"xt_{p}", [P, C, T], F32R) for p in ("hi", "lo")]
        ct = [sb(f"ct_{p}", [P, C, T], F32R) for p in ("hi", "lo")]
        acc = sb("acc", [P, TILES, D])
        raw_q, raw_k, raw_v = (sb(f"raw_{m}", [P, C, HG * DH]) for m in "qkv")
        raw_o = sb("raw_o", [P, HG, D])
        q_w, k_w, v_w = ([sb(f"w{m}_{p}", [P, C, HG * DH], F32R) for p in ("hi", "lo")] for m in "qkv")
        o_w = [sb(f"wo_{p}", [P, HG, D], F32R) for p in ("hi", "lo")]
        qt = [sb(f"qt_{p}", [P, BLK], F32R) for p in ("hi", "lo")]
        kt = sb("kt", [P, PB, 2, P], F32R)
        v = [[sb(f"v{b}_{p}", [P, PB, HG * DH], F32R) for p in ("hi", "lo")] for b in range(2)]
        ot = [sb(f"ot_{p}", [P, HG, BLK], F32R) for p in ("hi", "lo")]
        pt = sb("pt", [P, PB, 2, P], F32R)
        raw_bias = [sb(f"raw_bias{b}", [P, HG, PB, S]) for b in range(BLOCKS)]
        bias_m = [sb(f"bias_m{b}", [P, PB, S]) for b in range(2)]
        score = sb("score", [P, PB, S])
        shifted = sb("shifted", [P, PB, S])
        score_b = sb("score_b", [P, PB, S])
        attn = sb("attn", [P, BLK])
        expd = sb("expd", [P, PB, S])
        prob = sb("prob", [P, PB, P])
        row_max = sb("row_max", [P, PB])
        row_sum = sb("row_sum", [P, PB])
        row_inv = sb("row_inv", [P, PB])
        row_scale = sb("row_scale", [P, PB])
        mask_u8 = sb("mask_u8", [P, TILES, S], U8)
        mask_add = sb("mask_add", [P, TILES, S])
        row_kept = sb("row_kept", [P, TILES])
        raw_a = sb("raw_a", [P, C, P])
        raw_b = sb("raw_b", [P, D])
        a_w = [sb(f"a_{p}", [P, C, P], F32R) for p in ("hi", "lo")]
        b_w = [sb(f"b_{p}", [P, D], F32R) for p in ("hi", "lo")]
        stage = [sb(f"stage{i}", [P, 512]) for i in range(STAGE_BUFS)]
        xn = [sb(f"xn{i}", [P, D]) for i in range(2)]
        stats = sb("stats", [P, TILES, 6])
        mean_var = sb("mean_var", [P, TILES, 2])
        var_eps = sb("var_eps", [P, TILES])
        minus_half = sb("minus_half", [P, PB])
        rstd = sb("rstd", [P, TILES])
        lora_u = sb("lora_u", [P, BLK])
        y_out = [sb(f"y_out{i}", [P, D]) for i in range(2)]
        fb = sb("fb", [P, D])
        ident = sb("ident", [P, P])
        g_in = sb("g_in", [P, 2])
        gate = sb("gate", [P, 2])
        starts_i = sb("starts_i", [P, 4], I32)
        starts_f = sb("starts_f", [P, 4])
        lconst = sb("lconst", [P, NB + 1])
        seg = sb("seg", [P, NB])
        seg_j = sb("seg_j", [P, NB])
        use = sb("use", [P, NB])

        f_w = [c[:, :, BLK:T] for c in ct]
        lo_t = [[part[:, 2 * b:2 * b + 2, :].rearrange("p a b -> p (a b)") for part in v[1]] for b in range(BLOCKS)]

        q_bank, k_bank = pb("q_bank"), pb("k_bank")
        vo_bank = [pb(f"vo_bank{i}") for i in range(2)]
        s_two = ctx.enter_context(nc.psum_tensor("s_two", [P, PB, 2, P], F32))
        pv_two = ctx.enter_context(nc.psum_tensor("pv_two", [P, PB, 2, P], F32))
        s_half, pv_half = ([two[:, 2 * i:2 * i + 2, :, :].rearrange("p a b c -> p (a b c)") for i in range(2)]
                           for two in (s_two, pv_two))
        t_bank = pv_half[0]
        xt_bank = [[pv_half, vo_bank], [[q_bank, k_bank], pv_half]]
        y_bank = [q_bank, k_bank]
        l_bank = s_half

        raw_q_in, raw_k_in, raw_v_in, raw_o_in = (sem(f"raw_{m}_in") for m in "qkvo")
        bias_in = [sem(f"bias_in{b}") for b in range(BLOCKS)]
        x_in = [sem(f"x_in{i}") for i in range(TILES)]
        stage_in = [sem(f"stage_in{i}") for i in range(STAGE_BUFS)]
        mask_in, gate_in, fb_in, starts_in, const_in = (
            sem(f"{m}_in") for m in ("mask", "gate", "fb", "starts", "const"))
        stored = [sem(f"stored{i}") for i in range(2)]
        q_ps, k_ps, v_ps, s_ps, t_ps, pv_ps, o_ps, xt_ps, lora_ps, y_ps = (
            sem(f"{m}_ps") for m in ("q", "k", "v", "s", "t", "pv", "o", "xt", "lora", "y"))
        q_hi, k_hi, v_hi, pt_hi, ot_b, ot_hi, xt_hi, stage_hi, lora_hi, wq_hi, wk_hi, wv_hi, wo_hi = (
            sem(f"{m}_hi") for m in ("q", "k", "v", "pt", "ot_b", "ot", "xt", "stage", "lora", "wq", "wk", "wv", "wo"))
        q_lo, k_lo, v_lo, pt_lo, ot_lo, xt_lo, stage_lo, lora_lo, wq_lo, wk_lo, wv_lo, wo_lo = (
            sem(f"{m}_lo") for m in ("q", "k", "v", "pt", "ot", "xt", "stage", "lora", "wq", "wk", "wv", "wo"))
        gate_done, exp_done, var_done = sem("gate_done"), sem("exp_done"), sem("var_done")
        score_b_done, score_done, max_done, shift_done, sum_done, inv_done, rscale_done, prob_done = (
            sem(f"{m}_done") for m in ("score_b", "score", "max", "shift", "sum", "inv", "rscale", "prob"))
        ot_sum, acc_done, stats_done, aggr_done, rstd_done, xn_done, u_done, y_done = (
            sem(f"{m}_done") for m in ("ot_sum", "acc", "stats", "aggr", "rstd", "xn", "u", "y"))
        ident_done, zero_done, seg_done, mask_done, kept_done, half_done, fb_done = (
            sem(f"{m}_done") for m in ("ident", "zero", "seg", "mask", "kept", "half", "fb"))
        bias_done, yb_done = sem("bias_done"), sem("yb_done")
        lora_a_in, lora_b_in, g1_in = sem("lora_a_in"), sem("lora_b_in"), sem("g1_in")
        ab_hi, ab_lo = sem("ab_hi"), sem("ab_lo")

        def mm3(pe, to, left, right, first, last):
            pe.matmul(to, left[0], right[0], start=first, stop=False)
            pe.matmul(to, left[0], right[1], start=False, stop=False)
            return pe.matmul(to, left[1], right[0], start=False, stop=last)

        def parts(pair, *at):
            return [p[at] for p in pair]

        def cols(i, n):
            return slice(i * n, (i + 1) * n)

        def by(bank, n):
            return bank[:, :].rearrange("p (a b) -> p a b", a=n)

        def wait(eng, done, count):
            if not isinstance(count, int) or count > 0:
                eng.wait_ge(done, count)

        def both(pe, to, left, right):
            pe.matmul(to, left[0], right, start=True, stop=False)
            return pe.matmul(to, left[1], right, start=False, stop=True)

        def f32(part):
            return part.bitcast(F32)

        LAST = STAGES * G
        NOTHING = lambda: None

        block = ctx.enter_context(nc.Block())

        @block.sync
        def _(sp):
            def load(to, src, at, done):
                sp.dma_start(to, src[bass.ds(at, 1)].rearrange("a p f -> (a p) f")).then_inc(done, 16)

            def flat(t):
                return t[:, :, :].rearrange("p a b -> p (a b)")

            def flat4(t):
                return t[:, :, :, :].rearrange("p a b c -> p (a b c)")

            def load_x(half, i):
                wait(sp, y_done, TILES * (half - 1) + i + 1)
                load(acc[:, i, :], x, TILES * half + i, x_in[i])

            def load_piece(half, j):
                wait(sp, stage_lo, PIECES * half + j - STAGE_BUFS + 1)
                src, at = (ctxt, CTX_PIECES * half + j) if j < CTX_PIECES else (wf, j - CTX_PIECES)
                load(stage[j % STAGE_BUFS][:, :], src, at, stage_in[j % STAGE_BUFS])

            def next_group(gg, group, bias_at):
                for raw, src, w_hi, w_lo, arrived in ((raw_q, wq, wq_hi, wq_lo, raw_q_in),
                                                      (raw_k, wk, wk_hi, wk_lo, raw_k_in),
                                                      (raw_v, wv, wv_hi, wv_lo, raw_v_in)):
                    sp.wait_ge(w_hi, 2 * gg + 2)
                    sp.wait_ge(w_lo, 2 * gg + 2)
                    load(flat(raw), src, group, arrived)
                sp.wait_ge(bias_done, STAGES * gg + 2)
                load(flat4(raw_bias[0]), pair_bias, bias_at, bias_in[0])
                sp.wait_ge(wo_hi, 2 * gg + 2)
                sp.wait_ge(wo_lo, 2 * gg + 2)
                load(flat(raw_o), wo, group, raw_o_in)
                sp.wait_ge(bias_done, STAGES * gg + 4)
                load(flat4(raw_bias[1]), pair_bias, bias_at + 1, bias_in[1])

            for j in range(C):
                load_piece(0, j)
                load_x(0, j)
            for half in range(HALVES):
                if half:
                    sp.wait_ge(kept_done, half)
                    sp.wait_ge(mask_done, half)
                sp.dma_start(mask_u8[:, :, :], mask[half]).then_inc(mask_in, 16)
                if half == 0:
                    for i in range(PB, TILES):
                        load_x(0, i)
                for j in range(C, PIECES):
                    load_piece(half, j)
                with sp.Fori(0, G - 1) as g:
                    next_group(G * half + g, g + 1, g * BLOCKS + BLOCKS * (G * half + 1))
                if half < HALVES - 1:
                    next_group(G * half + (G - 1), 0, BLOCKS * G * (half + 1))
                    for j in range(C):
                        load_piece(half + 1, j)
                for i in range(TILES):
                    sp.wait_ge(y_done, TILES * half + i + 1)
                    sp.dma_start(out[TILES * half + i], y_out[i % 2][:, :]).then_inc(stored[i % 2], 16)
                    if half < HALVES - 1:
                        load_x(half + 1, i)
            for b in range(2):
                sp.wait_ge(stored[b], 16 * HALVES * TILES // 2)

        @block.tensor
        def _(pe):
            def queries_keys(gg, s):
                n, grp, h, tb = STAGES * gg + s, gg + s // STAGES, s % HG, s // 2 % BLOCKS
                for w, w_lo, src, bank, lo, done in ((q_w, wq_lo, xt, q_bank, q_lo, q_ps),
                                                     (k_w, wk_lo, ct, k_bank, k_lo, k_ps)):
                    pe.wait_ge(w_lo, 2 * grp + 1 + h)
                    wait(pe, lo, n)
                    for c in range(C):
                        mm = mm3(pe, bank[:, :], parts(w, slice(None), c, cols(h, DH)),
                                 parts(src, slice(None), c, cols(tb, BLK)), c == 0, c == C - 1)
                    mm.then_inc(done, 1)

            def values(gg, s, u):
                t, grp, tb = BLOCKS * gg + s // 2, gg + s // STAGES, s // 2 % BLOCKS
                if u == 0:
                    pe.wait_ge(wv_lo, 2 * grp + 2)
                    wait(pe, acc_done, PB * (t - 1))
                for i in range(2):
                    tile = PB * tb + 2 * u + i
                    for c in range(C):
                        mm = mm3(pe, vo_bank[u][:, cols(i, HG * DH)], parts(ct, slice(None), c, cols(tile, P)),
                                 parts(v_w, slice(None), c, slice(None)), c == 0, c == C - 1)
                mm.then_inc(v_ps, 1)

            def output(gg, s, u, values_before=True):
                t = BLOCKS * gg + s // 2 - 1
                if u == 0:
                    pe.wait_ge(ot_lo, HG * t + HG)
                    pe.wait_ge(wo_lo, 2 * (gg + (s // 2 - 1) // 2) + 2)
                for p in (2 * u, 2 * u + 1):
                    if p < 2 and values_before:
                        pe.wait_ge(v_lo, 2 * t + 3 + p)
                    else:
                        wait(pe, acc_done, PB * t + p - 1)
                    for h in range(HG):
                        mm = mm3(pe, vo_bank[p % 2][:, :], parts(ot, slice(None), h, cols(p, P)),
                                 parts(o_w, slice(None), h, slice(None)), h == 0, h == HG - 1)
                    mm.then_inc(o_ps, 1)

            def probabilities(n):
                pe.wait_ge(prob_done, n)
                wait(pe, ot_sum, n - 1)
                for p in range(PB):
                    mm = pe.transpose(t_bank[:, cols(p, P)], prob[:, p, :], ident[:, :])
                mm.then_inc(t_ps, 1)

            def scores(n):
                pe.wait_ge(q_lo, n + 1)
                pe.wait_ge(k_lo, n + 1)
                wait(pe, score_done, n)
                for p in range(PB):
                    mm = both(pe, s_two[:, p, :, :], parts(qt, slice(None), cols(p, P)), kt[:, p, :, :])
                mm.then_inc(s_ps, 1)

            def attention(gg, s):
                n, vb, vh = STAGES * gg + s, v[(s - 1) // 2 % 2], (s - 1) % HG
                pe.wait_ge(v_lo, 2 * (BLOCKS * gg + (s - 1) // 2) + 2)
                pe.wait_ge(pt_lo, n)
                for p in range(PB):
                    mm = both(pe, pv_two[:, p, :, :], parts(vb, slice(None), p, cols(vh, DH)), pt[:, p, :, :])
                mm.then_inc(pv_ps, 1)

            def slot(gg, s, output_before=True, before_scores=NOTHING):
                queries_keys(gg, s)
                if s % 2 == 0:
                    values(gg, s, 0)
                elif output_before:
                    output(gg, s, 0)
                probabilities(STAGES * gg + s)
                if s % 2 == 0:
                    values(gg, s, 1)
                elif output_before:
                    output(gg, s, 1)
                before_scores()
                scores(STAGES * gg + s)
                attention(gg, s)

            def transposes(half, norm, tiles):
                run = 2 * half + norm
                for i in tiles:
                    pe.wait_ge(xn_done, TILES * run + i + 1)
                    if i % PB >= 2:
                        pe.wait_ge(xt_lo, TILES * run + i - 1)
                    bank = xt_bank[norm][i // PB][i % 2]
                    for c in range(C):
                        mm = pe.transpose(bank[:, cols(c, P)], xn[i % 2][:, cols(c, P)], ident[:, :])
                    mm.then_inc(xt_ps, 1)

            def lora_inner(half, b):
                pe.wait_ge(xt_lo, TILES * (2 * half + 1) + PB * (b + 1))
                for c in range(C):
                    mm = mm3(pe, l_bank[b], parts(a_w, slice(None), c, slice(None)),
                             parts(xt, slice(None), c, cols(b, BLK)), c == 0, c == C - 1)
                mm.then_inc(lora_ps, 1)

            def dense(half, tiles):
                for i in tiles:
                    wait(pe, y_done, TILES * half + i - 1)
                    for c in range(C):
                        mm3(pe, y_bank[i % 2][:, :], parts(xt, slice(None), c, cols(i, P)),
                            parts(f_w, slice(None), c, slice(None)), c == 0, False)
                    pe.wait_ge(lora_lo, BLOCKS * half + i // PB + 1)
                    mm3(pe, y_bank[i % 2][:, :], parts(lo_t[i // PB], slice(None), cols(i % PB, P)),
                        parts(b_w, slice(None), slice(None)), False, True).then_inc(y_ps, 1)

            pe.wait_ge(ident_done, 2)
            for half in range(HALVES):
                first = G * half
                pe.wait_ge(stage_lo, PIECES * half + C)
                values(first, 0, 0)
                values(first, 0, 1)
                transposes(half, 0, range(PB))
                pe.wait_ge(xt_lo, 2 * TILES * half + PB)
                queries_keys(first, 0)
                scores(LAST * half)
                slot(first, 1, output_before=False,
                     before_scores=lambda: (pe.wait_ge(v_lo, 2 * BLOCKS * first + 2), transposes(half, 0, range(PB, TILES))))
                pe.wait_ge(stage_lo, PIECES * half + CTX_PIECES)
                pe.wait_ge(xt_lo, 2 * TILES * half + TILES)
                for s in range(2, STAGES + 2):
                    slot(first, s)
                with pe.Fori(1, G - 1) as g:
                    for s in range(2, STAGES + 2):
                        slot(g + first, s)
                slot(first + G - 1, 2)
                slot(first + G - 1, 3)
                n = LAST * (half + 1)
                pe.wait_ge(q_lo, n)
                pe.wait_ge(k_lo, n)
                transposes(half, 1, range(0, 2))
                probabilities(n)
                transposes(half, 1, range(2, PB))
                attention(first + G - 1, STAGES)
                pe.wait_ge(ab_lo, 2)
                pe.wait_ge(score_done, n)
                lora_inner(half, 0)
                output(first + G - 1, STAGES + 1, 0, values_before=False)
                output(first + G - 1, STAGES + 1, 1, values_before=False)
                pe.wait_ge(stage_lo, PIECES * (half + 1))
                pe.wait_ge(xt_lo, TILES * (2 * half + 1) + PB)
                dense(half, range(0, 2))
                pe.wait_ge(ot_sum, n)
                transposes(half, 1, range(PB, PB + 2))
                dense(half, range(2, 3))
                transposes(half, 1, range(PB + 2, TILES))
                dense(half, range(3, PB))
                lora_inner(half, 1)
                dense(half, range(PB, TILES))

        @block.scalar
        def _(act):
            def hi(to, src, done, func=ACT.Copy, **kw):
                act.activation(to, src, func, **kw).then_inc(done, 1)

            def weights_qk(grp, h):
                for raw, arrived, to, ps, done in ((raw_q, raw_q_in, q_w, q_ps, wq_hi),
                                                   (raw_k, raw_k_in, k_w, k_ps, wk_hi)):
                    act.wait_ge(arrived, 16 * (grp + 1))
                    if h == 1:
                        wait(act, ps, STAGES * grp)
                    hi(to[0][:, :, cols(h, DH)], raw[:, :, cols(h, DH)], done)

            def weights_v(grp):
                act.wait_ge(raw_v_in, 16 * (grp + 1))
                for u in range(2):
                    hi(v_w[0][:, cols(u, 2), :], raw_v[:, cols(u, 2), :], wv_hi)

            def weights_o(grp):
                act.wait_ge(raw_o_in, 16 * (grp + 1))
                wait(act, o_ps, BLOCKS * PB * grp)
                for u in range(HG):
                    hi(o_w[0][:, u, :], raw_o[:, u, :], wo_hi, scale=gate[:, 0:1])

            def queries_keys(n):
                wait(act, s_ps, n)
                act.wait_ge(q_ps, n + 1)
                hi(qt[0][:, :], q_bank[:, :], q_hi)
                act.wait_ge(k_ps, n + 1)
                hi(kt[:, :, 0, :], by(k_bank, PB), k_hi)

            def values(gg, s, u):
                t, tb = BLOCKS * gg + s // 2, s // 2 % BLOCKS
                wait(act, pv_ps, 2 * (t - 1))
                act.wait_ge(v_ps, 2 * t + 1 + u)
                hi(v[tb][0][:, cols(u, 2), :], by(vo_bank[u], 2), v_hi)

            def probabilities(n):
                wait(act, pv_ps, n - 1)
                act.wait_ge(t_ps, n)
                hi(pt[:, :, 0, :], by(t_bank, PB), pt_hi)

            def attention(gg, s):
                n = STAGES * gg + s
                wait(act, ot_lo, n - 1)
                act.wait_ge(pv_ps, n)
                act.activation(by(attn, PB), pv_two[:, :, 1, :], ACT.Copy).then_inc(ot_b, 1)
                wait(act, o_ps, PB * (BLOCKS * gg + (s - 1) // 2))
                act.wait_ge(ot_sum, n)
                hi(ot[0][:, (s - 1) % HG, :], attn[:, :], ot_hi)

            def exps(n):
                wait(act, sum_done, n)
                wait(act, prob_done, n)
                act.wait_ge(shift_done, n + 1)
                hi(expd[:, :, :], shifted[:, :, :], exp_done, ACT.Exp)

            def slot(gg, s, next_weights=True, after_probabilities=NOTHING):
                n, grp = STAGES * gg + s, gg + s // STAGES
                queries_keys(n)
                if s % STAGES == 0:
                    weights_qk(grp, 1)
                if s % STAGES == 2:
                    if next_weights:
                        weights_qk(grp + 1, 0)
                    weights_o(grp)
                if s % STAGES == 3 and next_weights:
                    weights_v(grp + 1)
                if s % 2 == 0:
                    values(gg, s, 0)
                probabilities(n)
                if s % 2 == 0:
                    values(gg, s, 1)
                after_probabilities()
                attention(gg, s)
                exps(n)

            def turned(half, norm, tiles):
                for i in tiles:
                    act.wait_ge(xt_ps, TILES * (2 * half + norm) + i + 1)
                    hi(xt[0][:, :, cols(i, P)], by(xt_bank[norm][i // PB][i % 2], C), xt_hi)

            def pieces(half, js):
                for j in js:
                    act.wait_ge(stage_in[j % STAGE_BUFS], 16 * (PIECES // STAGE_BUFS * half + j // STAGE_BUFS + 1))
                    raw = stage[j % STAGE_BUFS][:, :]
                    if j < CTX_PIECES:
                        hi(ct[0][:, j % C, cols(j // C, BLK)], raw, stage_hi)
                    else:
                        hi(f_w[0][:, j - CTX_PIECES, :], raw, stage_hi, scale=gate[:, 1:2])

            def lora(half, b):
                act.wait_ge(u_done, BLOCKS * half + b + 1)
                hi(lo_t[b][0], lora_u[:, :], lora_hi)

            def load(to, src, done):
                act.dma_start(to, src).then_inc(done, 16)

            load(raw_v[:, :, :].rearrange("p a b -> p (a b)"), wv[0], raw_v_in)
            load(raw_q[:, :, :].rearrange("p a b -> p (a b)"), wq[0], raw_q_in)
            load(raw_k[:, :, :].rearrange("p a b -> p (a b)"), wk[0], raw_k_in)
            load(g_in[:, 0:1], g_xattn.to_broadcast([P, 1]), gate_in)
            load(g_in[:, 1:2], g_ffn.to_broadcast([P, 1]), g1_in)
            load(raw_bias[0][:, :, :, :].rearrange("p a b c -> p (a b c)"), pair_bias[0], bias_in[0])
            load(raw_bias[1][:, :, :, :].rearrange("p a b c -> p (a b c)"), pair_bias[1], bias_in[1])
            load(raw_o[:, :, :].rearrange("p a b -> p (a b)"), wo[0], raw_o_in)
            load(starts_i[:, :], lora_starts.to_broadcast([P, NL + 1]), starts_in)
            load(lconst[:, :], lora_const, const_in)
            load(fb[:, :], fbias.to_broadcast([P, D]), fb_in)
            act.wait_ge(zero_done, 3)
            load(raw_a[:, :, 0:NL * R], lora_a, lora_a_in)
            load(raw_b[0:NL * R, :], lora_b, lora_b_in)
            pieces(0, range(C))
            weights_v(0)
            weights_qk(0, 0)
            for half in range(HALVES):
                first = G * half
                values(first, 0, 0)
                values(first, 0, 1)
                turned(half, 0, range(PB))
                queries_keys(LAST * half)
                if half == 0:
                    act.wait_ge(gate_in, 16)
                    act.wait_ge(g1_in, 16)
                    act.activation(gate[:, :], g_in[:, :], ACT.Tanh).then_inc(gate_done, 1)
                weights_qk(first, 1)
                pieces(half, range(C, CTX_PIECES))
                exps(LAST * half)
                if half == 0:
                    act.wait_ge(gate_done, 1)
                    act.wait_ge(lora_a_in, 16)
                    hi(a_w[0][:, :, :], raw_a[:, :, :], ab_hi)
                    act.wait_ge(lora_b_in, 16)
                    hi(b_w[0][:, :], raw_b[:, :], ab_hi, scale=gate[:, 1:2])
                slot(first, 1, after_probabilities=lambda: turned(half, 0, range(PB, TILES)))
                for s in range(2, STAGES + 2):
                    slot(first, s)
                with act.Fori(1, G - 1) as g:
                    for s in range(2, STAGES + 2):
                        slot(g + first, s)
                more = half < HALVES - 1
                slot(first + G - 1, 2, next_weights=more)
                slot(first + G - 1, 3, next_weights=more)
                n = LAST * (half + 1)
                act.wait_ge(k_ps, n)
                act.wait_ge(v_ps, n)
                turned(half, 1, range(0, 2))
                probabilities(n)
                turned(half, 1, range(2, PB))
                pieces(half, range(CTX_PIECES, CTX_PIECES + 2))
                attention(first + G - 1, STAGES)
                pieces(half, range(CTX_PIECES + 2, PIECES))
                lora(half, 0)
                if more:
                    pieces(half + 1, range(C))
                turned(half, 1, range(PB, TILES))
                lora(half, 1)
                act.wait_ge(y_ps, TILES * (half + 1))

        @block.vector
        def _(dve):
            def lo(to, src, of, done):
                dve.tensor_tensor(to, src, f32(of), ALU.subtract).then_inc(done, 1)

            def lo_scaled(to, src, scale, of, done):
                dve.scalar_tensor_tensor(out=to, in0=src, scalar=scale, in1=f32(of), op0=ALU.mult,
                                         op1=ALU.subtract).then_inc(done, 1)

            def queries_keys(n):
                dve.wait_ge(q_hi, n + 1)
                lo(qt[1][:, :], q_bank[:, :], qt[0][:, :], q_lo)
                dve.wait_ge(k_hi, n + 1)
                lo(kt[:, :, 1, :], by(k_bank, PB), kt[:, :, 0, :], k_lo)

            def weights_o(grp):
                for u in range(HG):
                    dve.wait_ge(wo_hi, 2 * grp + 1 + u)
                    lo_scaled(o_w[1][:, u, :], raw_o[:, u, :], gate[:, 0:1], o_w[0][:, u, :], wo_lo)

            def values(gg, s, u):
                t, tb = BLOCKS * gg + s // 2, s // 2 % BLOCKS
                dve.wait_ge(v_hi, 2 * t + 1 + u)
                lo(v[tb][1][:, cols(u, 2), :], by(vo_bank[u], 2), v[tb][0][:, cols(u, 2), :], v_lo)

            def output(gg, s, u):
                t = BLOCKS * gg + s // 2 - 1
                if u == 0:
                    wait(dve, acc_done, PB * t)
                for p in (2 * u, 2 * u + 1):
                    dve.wait_ge(o_ps, PB * t + p + 1)
                    tile = PB * ((s // 2 - 1) % BLOCKS) + p
                    dve.tensor_tensor(acc[:, tile, :], vo_bank[p % 2][:, :], acc[:, tile, :],
                                      ALU.add).then_inc(acc_done, 1)

            def probabilities(n):
                dve.wait_ge(pt_hi, n)
                lo(pt[:, :, 1, :], by(t_bank, PB), pt[:, :, 0, :], pt_lo)

            def scores(n, s):
                dve.wait_ge(bias_done, n + 1)
                wait(dve, shift_done, n)
                dve.wait_ge(s_ps, n + 1)
                for part, to, plus, done in ((1, score_b, bias_m[s % 2], score_b_done),
                                             (0, score, score_b, score_done)):
                    for b in range(2):
                        rows = cols(b, S)
                        last = dve.scalar_tensor_tensor(out=to[rows, :, :], in0=s_two[rows, :, part, rows],
                                                        scalar=SCALE, in1=plus[rows, :, :],
                                                        op0=ALU.mult, op1=ALU.add)
                    last.then_inc(done, 1)
                    dve.wait_ge(done, n + 1)
                dve.tensor_reduce(row_max[:, :], score[:, :, :], X, ALU.max).then_inc(max_done, 1)

            def attention(n):
                dve.wait_ge(ot_b, n)
                dve.tensor_tensor(by(attn, PB), pv_two[:, :, 0, :], by(attn, PB), ALU.add).then_inc(ot_sum, 1)

            def row_scales(n, tb):
                dve.wait_ge(exp_done, n + 1)
                dve.tensor_reduce(row_sum[:, :], expd[:, :, :], X, ALU.add).then_inc(sum_done, 1)
                dve.wait_ge(sum_done, n + 1)
                dve.reciprocal(row_inv[:, :], row_sum[:, :]).then_inc(inv_done, 1)
                dve.wait_ge(inv_done, n + 1)
                dve.tensor_tensor(row_scale[:, :], row_inv[:, :], row_kept[:, cols(tb, PB)],
                                  ALU.mult).then_inc(rscale_done, 1)

            def slot(gg, s, output_before=True, after_probabilities=NOTHING, before_scores=NOTHING, before_sums=NOTHING):
                n, tb = STAGES * gg + s, s // 2 % BLOCKS
                queries_keys(n)
                if s % STAGES == 2:
                    weights_o(gg + s // STAGES)
                if s % 2 == 0:
                    values(gg, s, 0)
                elif output_before:
                    output(gg, s, 0)
                probabilities(n)
                after_probabilities()
                if s % 2 == 0:
                    values(gg, s, 1)
                elif output_before:
                    output(gg, s, 1)
                before_scores()
                scores(n, s)
                attention(n)
                before_sums()
                row_scales(n, tb)

            def statistics(half, norm, b):
                run, tiles = 2 * half + norm, range(PB * b, PB * b + PB)
                for i in tiles:
                    if norm == 0:
                        dve.wait_ge(x_in[i], 16 * (half + 1))
                    dve.bn_stats(stats[:, i, :], acc[:, i, :]).then_inc(stats_done, 1)
                dve.wait_ge(stats_done, TILES * run + PB * (b + 1))
                for i in tiles:
                    dve.bn_aggr(mean_var[:, i, :], stats[:, i, :]).then_inc(aggr_done, 1)

            def normalise(half, norm, tiles):
                run = 2 * half + norm
                for i in tiles:
                    dve.wait_ge(rstd_done, BLOCKS * run + i // PB + 1)
                    wait(dve, xt_ps, TILES * run + i - 1)
                    dve.tensor_scalar(xn[i % 2][:, :], acc[:, i, :], mean_var[:, i, 0:1], rstd[:, i:i + 1],
                                      ALU.subtract, ALU.mult).then_inc(xn_done, 1)

            def turned(half, norm, tiles):
                for i in tiles:
                    dve.wait_ge(xt_hi, TILES * (2 * half + norm) + i + 1)
                    lo(xt[1][:, :, cols(i, P)], by(xt_bank[norm][i // PB][i % 2], C), xt[0][:, :, cols(i, P)], xt_lo)

            def pieces(half, js):
                for j in js:
                    dve.wait_ge(stage_hi, PIECES * half + j + 1)
                    raw = stage[j % STAGE_BUFS][:, :]
                    if j < CTX_PIECES:
                        at = (slice(None), j % C, cols(j // C, BLK))
                        lo(ct[1][at], raw, ct[0][at], stage_lo)
                    else:
                        c = j - CTX_PIECES
                        lo_scaled(f_w[1][:, c, :], raw, gate[:, 1:2], f_w[0][:, c, :], stage_lo)

            def lora(half, b):
                dve.wait_ge(lora_ps, BLOCKS * half + b + 1)
                dve.wait_ge(seg_done, 2 * NL + 3)
                batches = use[:, cols((TILES * half + PB * b) // PB, 2 * PB)]
                dve.tensor_tensor(lora_u[:, :].rearrange("p (b s) -> p b s", b=2 * PB), by(l_bank[b], 2 * PB),
                                  batches.unsqueeze(2).to_broadcast([P, 2 * PB, S]), ALU.mult).then_inc(u_done, 1)
                dve.wait_ge(lora_hi, BLOCKS * half + b + 1)
                lo(lo_t[b][1], lora_u[:, :], lo_t[b][0], lora_lo)

            def result(half, tiles):
                for i in tiles:
                    dve.wait_ge(y_ps, TILES * half + i + 1)
                    dve.wait_ge(yb_done, TILES * half + i + 1)
                    wait(dve, stored[i % 2], 16 * (TILES // 2 * half + i // 2))
                    dve.tensor_tensor(y_out[i % 2][:, :], y_bank[i % 2][:, :], acc[:, i, :],
                                      ALU.add).then_inc(y_done, 1)

            def constants():
                dve.wait_ge(gate_done, 1)
                dve.wait_ge(fb_in, 16)
                dve.tensor_scalar(fb[:, :], fb[:, :], gate[:, 1:2], None, ALU.mult).then_inc(fb_done, 1)
                dve.wait_ge(starts_in, 16)
                dve.wait_ge(const_in, 16)
                dve.tensor_copy(starts_f[:, :], starts_i[:, :]).then_inc(seg_done, 1)
                dve.wait_ge(seg_done, 1)
                dve.tensor_scalar(seg[:, :], lconst[:, 0:NB], starts_f[:, 0:1], None, ALU.is_ge).then_inc(seg_done, 1)
                for j in range(1, NL + 1):
                    dve.wait_ge(seg_done, 2 * j)
                    dve.tensor_scalar(seg_j[:, :], lconst[:, 0:NB], starts_f[:, j:j + 1], None,
                                      ALU.is_ge).then_inc(seg_done, 1)
                    dve.wait_ge(seg_done, 2 * j + 1)
                    dve.tensor_tensor(seg[:, :], seg[:, :], seg_j[:, :], ALU.add).then_inc(seg_done, 1)
                dve.wait_ge(seg_done, 2 * NL + 2)
                dve.tensor_scalar(use[:, :], seg[:, :], lconst[:, NB:NB + 1], None, ALU.is_equal).then_inc(seg_done, 1)
                dve.wait_ge(ab_hi, 1)
                lo(a_w[1][:, :, :], raw_a[:, :, :], a_w[0][:, :, :], ab_lo)
                dve.wait_ge(ab_hi, 2)
                lo_scaled(b_w[1][:, :], raw_b[:, :], gate[:, 1:2], b_w[0][:, :], ab_lo)

            dve.memset(minus_half[:, :], -0.5).then_inc(half_done, 1)
            dve.memset(prob[:, :, :], 0.0).then_inc(zero_done, 1)
            dve.memset(raw_a[:, :, :], 0.0).then_inc(zero_done, 1)
            dve.memset(raw_b[:, :], 0.0).then_inc(zero_done, 1)
            pieces(0, range(C))
            statistics(0, 0, 0)
            for half in range(HALVES):
                first = G * half
                normalise(half, 0, range(0, 2))
                values(first, 0, 0)
                values(first, 0, 1)
                turned(half, 0, range(0, 2))
                normalise(half, 0, range(2, PB))
                turned(half, 0, range(2, PB))
                queries_keys(LAST * half)
                dve.wait_ge(mask_in, 16 * (half + 1))
                dve.tensor_reduce(row_kept[:, :], mask_u8[:, :, :], X, ALU.max).then_inc(kept_done, 1)
                dve.wait_ge(kept_done, half + 1)
                scores(LAST * half, 0)
                statistics(half, 0, 1)
                row_scales(LAST * half, 0)
                pieces(half, range(C, CTX_PIECES))
                normalise(half, 0, range(PB, PB + 2))

                def block_1():
                    turned(half, 0, range(PB, PB + 2))
                    normalise(half, 0, range(PB + 2, TILES))
                    turned(half, 0, range(PB + 2, TILES))

                slot(first, 1, output_before=False, after_probabilities=block_1)
                if half == 0:
                    constants()
                for s in range(2, STAGES + 2):
                    slot(first, s)
                with dve.Fori(1, G - 1) as g:
                    for s in range(2, STAGES + 2):
                        slot(g + first, s)
                slot(first + G - 1, 2)
                n, end = LAST * (half + 1), first + G - 1

                def sums_of_block_0():
                    dve.wait_ge(acc_done, PB * (BLOCKS * (first + G) - 1))
                    statistics(half, 1, 0)

                slot(end, 3, before_scores=sums_of_block_0, before_sums=lambda: normalise(half, 1, range(0, 2)))
                turned(half, 1, range(0, 2))
                normalise(half, 1, range(2, PB))
                probabilities(n)
                turned(half, 1, range(2, PB))
                pieces(half, range(CTX_PIECES, CTX_PIECES + 2))
                attention(n)
                pieces(half, range(CTX_PIECES + 2, PIECES))
                lora(half, 0)
                output(end, STAGES + 1, 0)
                output(end, STAGES + 1, 1)
                dve.wait_ge(acc_done, PB * BLOCKS * (first + G))
                statistics(half, 1, 1)
                result(half, range(0, 1))
                normalise(half, 1, range(PB, PB + 2))
                result(half, range(1, 2))
                turned(half, 1, range(PB, PB + 2))
                normalise(half, 1, range(PB + 2, TILES))
                result(half, range(2, 3))
                turned(half, 1, range(PB + 2, TILES))
                result(half, range(3, PB))
                if half < HALVES - 1:
                    pieces(half + 1, range(C))
                lora(half, 1)
                result(half, range(PB, PB + 1))
                if half < HALVES - 1:
                    statistics(half + 1, 0, 0)
                result(half, range(PB + 1, TILES))

        @block.gpsimd
        def _(pool):
            def lo(to, src, of, done):
                pool.tensor_tensor(to, src, f32(of), ALU.subtract).then_inc(done, 1)

            def weights_qk(grp, h):
                for raw, w, w_hi, w_lo in ((raw_q, q_w, wq_hi, wq_lo), (raw_k, k_w, wk_hi, wk_lo)):
                    pool.wait_ge(w_hi, 2 * grp + 1 + h)
                    at = (slice(None), slice(None), cols(h, DH))
                    lo(w[1][at], raw[at], w[0][at], w_lo)

            def weights_v(grp):
                for u in range(2):
                    pool.wait_ge(wv_hi, 2 * grp + 1 + u)
                    lo(v_w[1][:, cols(u, 2), :], raw_v[:, cols(u, 2), :], v_w[0][:, cols(u, 2), :], wv_lo)

            def deviations(half, norm, b):
                run = 2 * half + norm
                pool.wait_ge(half_done, 1)
                pool.wait_ge(aggr_done, TILES * run + PB * (b + 1))
                pool.tensor_scalar(var_eps[:, cols(b, PB)], mean_var[:, cols(b, PB), 1], EPS, None,
                                   ALU.add).then_inc(var_done, 1)
                pool.wait_ge(var_done, BLOCKS * run + b + 1)
                pool.tensor_tensor(rstd[:, cols(b, PB)], var_eps[:, cols(b, PB)], minus_half[:, :],
                                   ALU.pow).then_inc(rstd_done, 1)

            def attention_lo(n, s):
                pool.wait_ge(ot_hi, n)
                lo(ot[1][:, (s - 1) % HG, :], attn[:, :], ot[0][:, (s - 1) % HG, :], ot_lo)

            def slot(gg, s, first=False, next_weights=True, before_shift=NOTHING, before_probabilities=NOTHING):
                n, grp, tb = STAGES * gg + s, gg + s // STAGES, s // 2 % BLOCKS
                wait(pool, prob_done, n)
                pool.wait_ge(bias_in[tb], 16 * (grp + 1))
                wait(pool, score_done, n - 1)
                pool.tensor_tensor(bias_m[s % 2][:, :, :], raw_bias[tb][:, s % HG, :, :],
                                   mask_add[:, cols(tb, PB), :], ALU.add).then_inc(bias_done, 1)
                if s % STAGES == 0:
                    weights_qk(grp, 1)
                if s % STAGES == 2 and next_weights:
                    weights_qk(grp + 1, 0)
                if s % STAGES == 3 and next_weights:
                    weights_v(grp + 1)
                before_shift()
                wait(pool, exp_done, n)
                pool.wait_ge(max_done, n + 1)
                pool.tensor_tensor(shifted[:, :, :], score[:, :, :],
                                   row_max[:, :].unsqueeze(2).to_broadcast([P, PB, S]),
                                   ALU.subtract).then_inc(shift_done, 1)
                before_probabilities()
                if not first:
                    attention_lo(n, s)
                    pool.wait_ge(ot_lo, n)
                wait(pool, t_ps, n)
                pool.wait_ge(rscale_done, n + 1)
                for b in range(2):
                    rows = cols(b, S)
                    last = pool.tensor_tensor(prob[rows, :, rows], expd[rows, :, :],
                                              row_scale[rows, :].unsqueeze(2).to_broadcast([S, PB, S]), ALU.mult)
                last.then_inc(prob_done, 1)

            def add_bias(half, tiles):
                for i in tiles:
                    pool.wait_ge(xn_done, TILES * (2 * half + 1) + i + 1)
                    pool.tensor_tensor(acc[:, i, :], acc[:, i, :], fb[:, :], ALU.add).then_inc(yb_done, 1)

            pool.memset(ident[:, :], 0.0).then_inc(ident_done, 1)
            pool.wait_ge(ident_done, 1)
            pool.affine_select(out=ident[:, :], in_=ident[:, :], compare_op=ALU.not_equal, fill=1.0, base=0,
                               pattern=[[-1, P]], channel_multiplier=1).then_inc(ident_done, 1)
            weights_v(0)
            deviations(0, 0, 0)
            weights_qk(0, 0)
            pool.wait_ge(zero_done, 1)
            for half in range(HALVES):
                first = G * half
                pool.wait_ge(mask_in, 16 * (half + 1))
                pool.tensor_scalar(mask_add[:, :, :], mask_u8[:, :, :], -1.0, -MASKED, ALU.add,
                                   ALU.mult).then_inc(mask_done, 1)
                pool.wait_ge(mask_done, half + 1)

                def deviations_1():
                    deviations(half, 0, 1)
                    pool.wait_ge(rstd_done, BLOCKS * 2 * half + 2)

                slot(first, 0, first=True, before_probabilities=deviations_1)
                for s in range(1, STAGES + 2):
                    slot(first, s)
                with pool.Fori(1, G - 1) as g:
                    for s in range(2, STAGES + 2):
                        slot(g + first, s)
                more = half < HALVES - 1
                slot(first + G - 1, 2, next_weights=more)
                slot(first + G - 1, 3, next_weights=more, before_shift=lambda: deviations(half, 1, 0))
                n = LAST * (half + 1)
                pool.wait_ge(prob_done, n)
                attention_lo(n, STAGES)
                pool.wait_ge(fb_done, 1)
                add_bias(half, range(PB))
                deviations(half, 1, 1)
                add_bias(half, range(PB, TILES))
                if more:
                    deviations(half + 1, 0, 0)


_OUTS = [((NB, S, D), "float32")]


def kernel(**inputs):
    import numpy as _np
    import concourse.bacc as _bacc
    from concourse import mybir as _mybir
    from concourse.bass_utils import run_bass_kernel_spmd as _run

    a = {k: _np.asarray(v) for k, v in inputs.items()}

    def by_group(w):
        return w.reshape(C, P, G, HG * DH).transpose(2, 1, 0, 3).reshape(G, P, C * HG * DH)

    bias = a["fside_Bx32xSxS2_0"].reshape(HALVES, BLOCKS, PB, 2, G, HG, S, S)
    mask = a["mask_BxSxS2_bk0"].reshape(HALVES, TILES, 2, S, S)
    arrays = {
        "x": a["x"].reshape(HALVES * TILES, P, D),
        "ctxt": a["ctx_4096"].reshape(HALVES, BLOCKS, BLK, C, P).transpose(0, 1, 3, 4, 2).reshape(-1, P, BLK),
        "pair_bias": bias.transpose(0, 4, 1, 3, 6, 5, 2, 7).reshape(HALVES * G * BLOCKS, P, HG * PB * S),
        "mask": mask.transpose(0, 2, 3, 1, 4).reshape(HALVES, P, TILES, S),
        "wq": by_group(a["L0_xattn_Wq"]),
        "wk": by_group(a["L0_xattn_Wk"]),
        "wv": by_group(a["L0_xattn_Wv"]),
        "wo": a["L0_xattn_Wo"].reshape(G, HG, DH, D).transpose(0, 2, 1, 3).reshape(G, P, HG * D),
        "g_xattn": a["g_xattn"].reshape(1, 1),
        "g_ffn": a["g_ffn"].reshape(1, 1),
        "wf": a["L0_ffn_weight"].T.reshape(C, P, D),
        "fbias": a["L0_ffn_bias"].reshape(1, D),
        "lora_a": a["L0_ffn_lora_A"].reshape(NL * R, C, P).transpose(2, 1, 0),
        "lora_b": a["L0_ffn_lora_B"].transpose(0, 2, 1).reshape(NL * R, D),
        "lora_starts": a["L0_ffn_lora_start_indices"].reshape(1, NL + 1),
        "lora_const": _np.concatenate([_np.tile(_np.arange(NB, dtype=_np.float32), (P, 1)),
                                       (_np.arange(P)[:, None] // R + 2).astype(_np.float32)], axis=1),
    }
    arrays = {f"in_{k}": _np.ascontiguousarray(v) for k, v in arrays.items()}
    nc = _bacc.Bacc("TRN2", target_bir_lowering=False, num_devices=1, dynamic_dma_scratch_size=1024)
    args = [nc.dram_tensor(k, v.shape, _mybir.dt.from_np(v.dtype), kind="ExternalInput").ap()
            for k, v in arrays.items()]
    args.append(nc.dram_tensor("out_0", (HALVES * TILES, P, D), _mybir.dt.float32, kind="ExternalOutput").ap())
    flamingo_block(nc, *args)
    r = _run(nc, [arrays], core_ids=[0])
    return r.results[0]["out_0"].reshape(_OUTS[0][0])
```
